# Optimizing a Trainium2 kernel written in Bass

```python
import numpy as np
import jax
import jax.numpy as jnp

def _softmax(x, axis=-1):
    return jax.nn.softmax(x, axis=axis)

def _gelu(x):
    return jax.nn.gelu(x, approximate=True)

def _silu(x):
    return jax.nn.silu(x)

def _sigmoid(x):
    return jax.nn.sigmoid(x)

def _layernorm(x, axis=-1, eps=1e-05):
    m = jnp.mean(x, axis=axis, keepdims=True)
    v = jnp.var(x, axis=axis, keepdims=True)
    return (x - m) / jnp.sqrt(v + eps)

def _scatter_add(tgt, idx, src, axis=0):
    return tgt.at[idx].add(src)

def _segment_sum(src, seg, n):
    return jax.ops.segment_sum(src, seg, n)
kernel_name = 'mk_macaron_d1_jaxref_r8_b7d470'

def setup_inputs(seed: int=0):
    np.random.seed(seed)
    _w = jnp.asarray

    def _L0_attn_setup():
        import jax, jax.numpy as jnp
        import numpy as np
        B, T, C = (4, 512, 128)
        H = 16
        D = C // H
        W_SCALE = 0.02
        key = jax.random.key(seed)
        ks = jax.random.split(key, 9)
        inp = {'x': jax.random.normal(ks[0], (B, T, C), dtype=jnp.float32)}
        for i, nm in enumerate(['q', 'k', 'v', 'o']):
            inp[f'W{nm}'] = jax.random.normal(ks[1 + i], (C, C), dtype=jnp.float32) * W_SCALE
            inp[f'b{nm}'] = jnp.zeros((C,), dtype=jnp.float32)
        return inp
    _L0_attn_in = _L0_attn_setup()

    def _L0_ffn_setup():
        import jax, jax.numpy as jnp
        import numpy as np
        E = 8
        K = 2
        CAP_FACTOR = 1.0
        key = jax.random.key(seed)
        k0, k1, k2, k3 = jax.random.split(key, 4)
        B, S, M, H = (4, 256, 128, 512)
        x = jax.random.normal(k0, (B, S, M), jnp.float32)
        wg = jax.random.normal(k1, (M, E), jnp.float32) * 0.02
        w1 = jax.random.normal(k2, (E, M, H), jnp.float32) * 0.02
        b1 = jnp.zeros((E, H), jnp.float32)
        w2 = jax.random.normal(k3, (E, H, M), jnp.float32) * 0.02
        b2 = jnp.zeros((E, M), jnp.float32)
        return {'x': x, 'wg': wg, 'w1': w1, 'b1': b1, 'w2': w2, 'b2': b2}
    _L0_ffn_in = _L0_ffn_setup()
    _d = {'L0_attn_x': _L0_attn_in['x'], 'L0_attn_Wq': _L0_attn_in['Wq'], 'L0_attn_bq': _L0_attn_in['bq'], 'L0_attn_Wk': _L0_attn_in['Wk'], 'L0_attn_bk': _L0_attn_in['bk'], 'L0_attn_Wv': _L0_attn_in['Wv'], 'L0_attn_bv': _L0_attn_in['bv'], 'L0_attn_Wo': _L0_attn_in['Wo'], 'L0_attn_bo': _L0_attn_in['bo'], 'L0_ffn_wg': _L0_ffn_in['wg'], 'L0_ffn_w1': _L0_ffn_in['w1'], 'L0_ffn_b1': _L0_ffn_in['b1'], 'L0_ffn_w2': _L0_ffn_in['w2'], 'L0_ffn_b2': _L0_ffn_in['b2']}
    _x0 = _d['L0_attn_x']
    _d['L0_attn_x'] = jax.random.normal(jax.random.fold_in(jax.random.key(seed), 1), (8, 512, 128), dtype=_x0.dtype)
    del _x0
    return _d

def reference(L0_attn_x, L0_attn_Wq, L0_attn_bq, L0_attn_Wk, L0_attn_bk, L0_attn_Wv, L0_attn_bv, L0_attn_Wo, L0_attn_bo, L0_ffn_wg, L0_ffn_w1, L0_ffn_b1, L0_ffn_w2, L0_ffn_b2):

    def _L0_attn_ref(x, Wq, bq, Wk, bk, Wv, bv, Wo, bo):
        import jax, jax.numpy as jnp
        import numpy as np
        B, T, C = (4, 512, 128)
        H = 16
        D = C // H
        W_SCALE = 0.02
        Bx, Tx, Cx = x.shape
        q = (x @ Wq.T + bq).reshape(Bx, Tx, H, D)
        k = (x @ Wk.T + bk).reshape(Bx, Tx, H, D)
        v = (x @ Wv.T + bv).reshape(Bx, Tx, H, D)
        q = jax.nn.elu(q) + 1.0
        k = jax.nn.elu(k) + 1.0
        kv = jnp.einsum('bthd,bthe->bhde', k, v)
        denom = jnp.einsum('bthd,bhd->bth', q, k.sum(axis=1))
        num = jnp.einsum('bthd,bhde->bthe', q, kv)
        out = num / jnp.clip(denom, 1e-06, None)[..., None]
        out = out.reshape(Bx, Tx, Cx)
        return out @ Wo.T + bo

    def _L0_ffn_ref(x, wg, w1, b1, w2, b2):
        import jax, jax.numpy as jnp
        import numpy as np
        E = 8
        K = 2
        CAP_FACTOR = 1.0
        B, S, M = x.shape
        N = B * S
        capacity = int(CAP_FACTOR * K * N // E)
        xt = x.reshape(N, M)
        logits = xt @ wg
        scores = jax.nn.softmax(logits, axis=-1)
        topv, topi = jax.lax.top_k(scores, K)
        topv = topv / jnp.sum(topv, axis=-1, keepdims=True)
        masks = jax.nn.one_hot(topi.T, E, dtype=jnp.int32)
        flat = masks.reshape(K * N, E)
        locs = jnp.cumsum(flat, axis=0) - 1
        pos = jnp.sum(locs * flat, axis=-1).reshape(K, N).T
        valid = pos < capacity
        gate = topv * valid.astype(topv.dtype)
        pos_c = jnp.where(valid, pos, 0)
        xk = xt[:, None, :] * valid[..., None].astype(xt.dtype)
        disp = jnp.zeros((E, capacity, M), xt.dtype)
        disp = disp.at[topi, pos_c].add(xk)
        h = jax.nn.relu(jnp.einsum('ecm,emh->ech', disp, w1) + b1[:, None, :])
        y = jnp.einsum('ech,ehm->ecm', h, w2) + b2[:, None, :]
        out = jnp.sum(gate[..., None] * y[topi, pos_c], axis=1)
        return out.reshape(B, S, M)
    x = L0_attn_x
    x = x + 0.5 * _L0_ffn_ref(_layernorm(x, axis=-1), L0_ffn_wg, L0_ffn_w1, L0_ffn_b1, L0_ffn_w2, L0_ffn_b2)
    x = x + _L0_attn_ref(_layernorm(x, axis=-1), L0_attn_Wq, L0_attn_bq, L0_attn_Wk, L0_attn_bk, L0_attn_Wv, L0_attn_bv, L0_attn_Wo, L0_attn_bo)
    x = x + 0.5 * _L0_ffn_ref(_layernorm(x, axis=-1), L0_ffn_wg, L0_ffn_w1, L0_ffn_b1, L0_ffn_w2, L0_ffn_b2)
    return x

_drawn_inputs = setup_inputs


def setup_inputs(seed=0):
    import zlib

    import numpy as np

    out = dict(_drawn_inputs(seed))
    spreads = {'L0_attn_bq': (0.0, 2.0),
     'L0_attn_bk': (0.0, 2.0),
     'L0_attn_bv': (0.0, 0.369),
     'L0_attn_bo': (0.0, 0.1),
     'L0_ffn_b1': (0.0, 0.381),
     'L0_ffn_b2': (0.0, 0.1)}
    factors = {'L0_attn_Wq': 37.826, 'L0_attn_Wk': 23.844, 'L0_attn_Wv': 8.0}
    for name, (base, spread) in spreads.items():
        noise = np.random.default_rng([zlib.crc32(name.encode()), seed]).standard_normal(out[name].shape)
        drawn = base * np.exp(spread * noise) if base else spread * noise
        out[name] = jnp.asarray(drawn.astype(out[name].dtype))
    for name, factor in factors.items():
        out[name] = (out[name] * factor).astype(out[name].dtype)
    return out
```

```python
import concourse.bass as bass
from concourse import mybir
from contextlib import ExitStack

F32 = mybir.dt.float32
F32R = mybir.dt.float32r
BF16 = mybir.dt.bfloat16
I32 = mybir.dt.int32
ALU = mybir.AluOpType
ACT = mybir.ActivationFunctionType
AX = mybir.AxisListType.X

P = 128
NB, SEQ, C = 8, 512, 128
N = NB * SEQ
NT = N // P
GT = SEQ // P
NG = NT // GT
E, K, H = 8, 2, 512
HC = H // P
CAP = K * N // E
NCH = CAP // P
NSB = E * CAP // 512
HEADS, HD = 16, 8
EPS = 1e-5
FAR = -3e38
RSQRT_SEED = 1597463007.0


class Chain:

    def __init__(self, eng, sem):
        self.eng, self.sem, self.n, self.turns = eng, sem, 0, 0

    def add(self, ins):
        ins.then_inc(self.sem, 1)
        self.n += 1

    def wait(self):
        self.eng.wait_ge(self.sem, self.turns + self.n)

    def then(self, ins):
        self.add(ins)
        self.wait()

    def enter(self, i, count):
        self.start, self.count, self.turns = self.n, count, i * count

    def leave(self, turns):
        assert self.n - self.start == self.count, (self.n - self.start, self.count)
        self.n, self.turns = self.start + turns * self.count, 0


def macaron(nc, x_in, Wq, bq, Wk, bk, Wv, bv, Wo, bo, wg, w1, b1, w2, b2, out):
    ctx = ExitStack()
    with ctx:
        def sb(name, shape, dt=F32):
            return ctx.enter_context(nc.sbuf_tensor(name, shape, dt))

        def scoped(stage, name, shape, dt=F32):
            return stage.enter_context(nc.sbuf_tensor(name, shape, dt))

        def sem(name):
            return ctx.enter_context(nc.semaphore(name))

        def sems(name, n):
            return [sem(f"{name}{i}") for i in range(n)]

        xf = x_in.rearrange("b s c -> (b s) c")
        of = out.rearrange("b s c -> (b s) c")
        xn_dram = nc.dram_tensor("xn_dram", (N, C), F32, kind="Internal").ap()
        y_dram = nc.dram_tensor("y_dram", (E * CAP, C), F32, kind="Internal").ap()

        def rows(dram, at, tiles=GT):
            return dram[bass.ds(at, tiles * P), :].rearrange("(t p) c -> p t c", p=P)

        ident = sb("ident", [P, P])
        tri = sb("tri", [P, P], BF16)
        ones_bf = sb("ones_bf", [P, P], BF16)
        iota_lo = sb("iota_lo", [P, P])
        prefer = sb("prefer", [P, E])
        iota_hi = sb("iota_hi", [P, NCH])
        expert_base = sb("expert_base", [P, E])
        token_id = sb("token_id", [P, NT])
        carry = sb("carry", [P, E, K * NT])
        head_mask = sb("head_mask", [P, HEADS])
        block_mask = sb("block_mask", [P, P])
        ones_row = sb("ones_row", [2, P])
        ones2 = sb("ones2", [2, P], F32R)
        part01 = sb("part01", [2, 2])
        wg_sb = sb("wg_sb", [P, E])
        WT = sb("WT", [P, 4, C])
        bcol = sb("bcol", [P, E * (HC + 1) + 1])
        nbq = sb("nbq", [P, 1])
        brow = sb("brow", [2, 3, C])
        bhi = sb("bhi", [2, 3, C], F32R)
        blo = sb("blo", [2, 3, C], F32R)
        bsum = sb("bsum", [2, 3, C])
        bpair = sb("bpair", [2, 3, C], F32R)
        wres = sb("wres", [P, E, 4, H], F32R)
        bst = [sb(f"bst{i}", [P, HC + 1]) for i in range(2)]
        wst = [sb(f"wst{i}", [P, 4, H], F32R) for i in range(2)]
        x_sb = sb("x_sb", [P, NT, C])
        stats = sb("stats", [P, NT, 6])
        mean = sb("mean", [P, NT])
        nw = sb("nw", [P, 5, NT])
        rstd = sb("rstd", [P, NT])
        nmr = sb("nmr", [P, NT])
        gate = sb("gate", [P, K, NT])
        slot = sb("slot", [P, K, NT], I32)
        gidx = sb("gidx", [P, E * NCH], I32)

        bank = [ctx.enter_context(nc.psum_tensor(f"bank{i}", [P, 512], F32)) for i in range(8)]

        consts = sem("consts")
        const_chain = sem("const_chain")
        small_in = sems("small_in", 3)
        x_arrived = sems("x_arrived", 2)
        stats_done = sems("stats_done", 2)
        exp_raw_in = sems("exp_raw_in", 2)
        exp_hi = sem("exp_hi")
        exp_lo = sem("exp_lo")
        WT_ps = sem("WT_ps")
        WT_sb = sem("WT_sb")
        bpair_done = sem("bpair_done")
        dve_step = sem("dve_step")
        act_step = sem("act_step")
        rstd_done = sem("rstd_done")
        norm_dve = sem("norm_dve")
        norm_act = sem("norm_act")
        turned = sems("turned", 2)
        xnT_out = sems("xnT_out", 2)
        logits_done = sems("logits_done", 2)
        xn_stored = sems("xn_stored", 2)
        gap_done = sem("gap_done")
        exp_gap = sem("exp_gap")
        onehot_done = sem("onehot_done")
        counts_done = sem("counts_done")
        lo_ready = sem("lo_ready")
        lo_used = sem("lo_used")
        inverse_done = sem("inverse_done")
        gathered = sems("gathered", 4)
        w_loaded = sems("w_loaded", 2)
        xT_ready = sem("xT_ready")
        xh_ready = sem("xh_ready")
        xl_ready = sem("xl_ready")
        h_ready = sems("h_ready", HC)
        hf_ready = sems("hf_ready", HC)
        hh_ready = sems("hh_ready", HC)
        hl_ready = sems("hl_ready", HC)
        up_done = sem("up_done")
        yT_ready = sem("yT_ready")
        ytr_ready = sem("ytr_ready")
        y_ready = sem("y_ready")
        y_stored = sems("y_stored", 2)
        yg_in = sems("yg_in", 2)
        yg_used = sems("yg_used", 2)
        out_stored = sems("out_stored", 2)

        def layer_norm_scalars(ch, dve, st, mean_ap, out_ap, nmr_ap, scratch):
            v, half, y, a = scratch
            ch.add(dve.tensor_tensor(a, st[:, :, 1], st[:, :, 4], ALU.subtract))
            ch.add(dve.tensor_tensor(y, st[:, :, 2], st[:, :, 5], ALU.add))
            ch.then(dve.tensor_tensor(half, st[:, :, 1], st[:, :, 4], ALU.add))
            ch.add(dve.tensor_tensor(a, a, a, ALU.mult))
            ch.then(dve.tensor_scalar(mean_ap, half, 0.5, None, ALU.mult))
            ch.then(dve.scalar_tensor_tensor(a, a, C / 4, y, ALU.mult, ALU.add))
            ch.then(dve.tensor_scalar(a, a, 1.0 / C, None, ALU.mult))
            var = a
            ch.add(dve.tensor_scalar(v, var, EPS, None, ALU.add))
            ch.then(dve.tensor_scalar(half, var, -0.5, -0.5 * EPS, ALU.mult, ALU.add))
            ch.then(dve.tensor_scalar(y.bitcast(I32), v.bitcast(I32), -0.5, RSQRT_SEED, ALU.mult, ALU.add))
            for turn in range(3):
                ch.then(dve.tensor_tensor(a, y, y, ALU.mult))
                ch.then(dve.tensor_tensor(a, a, half, ALU.mult))
                ch.then(dve.scalar_tensor_tensor(out_ap if turn == 2 else y, a, 1.5, y, ALU.add, ALU.mult))
            ch.then(dve.scalar_tensor_tensor(nmr_ap, mean_ap, -1.0, out_ap, ALU.mult, ALU.mult))

        NBIAS = E * HC + E + 1

        class Route:

            def __init__(self, f, stage):
                self.f = f
                new = lambda name, shape, dt=F32: scoped(stage, f"{name}_{f}", shape, dt)
                self.L = new("logits", [P, NT, E])
                self.w = new("ranked", [P, NT, E])
                self.m = new("first", [P, NT])
                self.m2 = new("second", [P, NT])
                self.top = new("top", [P, NT])
                self.gap = new("gap", [P, NT])
                self.e2 = new("exp_gap_sb", [P, NT])
                self.choice = new("choice", [P, E, K, NT], BF16)
                self.pos = new("pos", [P, E, K * NT])
                self.cum = new("cum", [P, E, K * NT])
                self.base = new("base", [P, K * NT])
                self.at = new("at", [P, K * NT])
                self.at_i = new("at_i", [P, K * NT], I32)
                self.valid = new("valid", [P, K * NT])
                self.slotf = new("slotf", [P, K * NT])
                self.lof = new("lof", [P, K * NT])
                self.hif = new("hif", [P, K * NT])
                self.hi_oh = new("hi_oh", [P, K * NT, NCH])
                self.hi_tok = new("hi_tok", [P, K * NT, E * NCH], F32R)
                self.lo = new("lo", [P, 8, P], F32R)
                self.xns = new("xns", [P, 2, GT, C])
                self.xnT = new("xnT", [P, 2, SEQ])

            def sync(self, sp):
                f = self.f
                with sp.Fori(0, NG // 2) as i:
                    for u in range(2):
                        g = 2 * i + u
                        sp.wait_ge(norm_dve, NG * f + g + 1)
                        sp.wait_ge(norm_act, NG * f + g + 1)
                        sp.dma_start(rows(xn_dram, g * SEQ), self.xns[:, u]).then_inc(xn_stored[u], 16)
                for e in range(2):
                    if f == 0:
                        sp.wait_ge(exp_lo, e + 1)
                    sp.dma_start(wst[e][:].bitcast(F32), wres[:, e].bitcast(F32)).then_inc(w_loaded[e], 16)
                    if f == 0:
                        sp.wait_ge(WT_sb, 2)
                    sp.dma_start(bst[e][:], bcol[:, e * (HC + 1):(e + 1) * (HC + 1)]).then_inc(w_loaded[e], 16)
                for u in range(2):
                    sp.wait_ge(xn_stored[u], 16 * NG // 2 * (f + 1))
                    sp.wait_ge(w_loaded[u], 32 * (E // 2 * f + 1))

            def scalar(self, act):
                f = self.f
                act.wait_ge(rstd_done, f + 1)
                with act.Fori(0, NG // 2) as i:
                    for u in range(2):
                        g = 2 * i + u
                        act.wait_ge(xn_stored[u], 16 * (NG // 2 * f + i))
                        act.wait_ge(turned[u], NG // 2 * f + i)
                        t = GT * g + GT - 1
                        nc.scalar.activation(self.xns[:, u, GT - 1], x_sb[:, bass.ds(t, 1), :].rearrange("p a c -> p (a c)"), ACT.Identity,
                                             bias=nmr[:, bass.ds(t, 1)], scale=rstd[:, bass.ds(t, 1)]).then_inc(norm_act, 1)
                    for u in range(2):
                        act.wait_ge(turned[u], NG // 2 * f + i + 1)
                        act.wait_ge(logits_done[u], NG // 2 * f + i)
                        nc.scalar.copy(self.xnT[:, u], bank[u][:]).then_inc(xnT_out[u], 1)
                act.wait_ge(gap_done, f + 1)
                nc.scalar.activation(self.e2[:], self.gap[:], ACT.Exp).then_inc(exp_gap, 1)

            def tensor(self, pe):
                f = self.f
                with pe.Fori(0, NG // 2) as i:
                    for u in range(2):
                        g = 2 * i + u
                        pe.wait_ge(norm_dve, NG * f + g + 1)
                        pe.wait_ge(norm_act, NG * f + g + 1)
                        pe.wait_ge(xnT_out[u], NG // 2 * f + i)
                        for t in range(GT):
                            last = nc.tensor.transpose(bank[u][:, t * P:(t + 1) * P], self.xns[:, u, t], ident[:])
                        last.then_inc(turned[u], 1)
                    for u in range(2):
                        g = 2 * i + u
                        pe.wait_ge(xnT_out[u], NG // 2 * f + i + 1)
                        for t in range(GT):
                            last = nc.tensor.matmul(bank[2][:, bass.ds((GT * g + t) * E, E)], self.xnT[:, u, t * P:(t + 1) * P],
                                                    wg_sb[:], start=True, stop=True)
                        last.then_inc(logits_done[u], 1)
                pe.wait_ge(onehot_done, f + 1)
                flat = self.choice[:].rearrange("p e k t -> p (e k t)")
                nc.tensor.matmul(bank[3][:], tri[:], flat, start=True, stop=True)
                nc.tensor.matmul(bank[4][:], ones_bf[:], flat, start=True, stop=True).then_inc(counts_done, 1)
                for j in range(K * NT):
                    pe.wait_ge(lo_ready, K * NT * f + j + 1)
                    nc.tensor.matmul(bank[5][:, 0:E * NCH], self.lo[:, j % 8], self.hi_tok[:, j],
                                     start=(j == 0), stop=(j == K * NT - 1)).then_inc(lo_used, 1)

            def vector(self, dve, ch):
                f = self.f
                layer_norm_scalars(ch, dve, stats, mean[:], rstd[:], nmr[:], [nw[:, q] for q in range(4)])
                dve.tensor_copy(nw[:, 4, 0:1], nmr[:, 0:1]).then_inc(rstd_done, 1)
                with dve.Fori(0, NG // 2) as i:
                    for u in range(2):
                        g = 2 * i + u
                        dve.wait_ge(xn_stored[u], 16 * (NG // 2 * f + i))
                        dve.wait_ge(turned[u], NG // 2 * f + i)
                        for tt in range(GT - 1):
                            t = GT * g + tt
                            last = dve.tensor_scalar(self.xns[:, u, tt], x_sb[:, bass.ds(t, 1), :].rearrange("p a c -> p (a c)"),
                                                     mean[:, bass.ds(t, 1)], rstd[:, bass.ds(t, 1)], ALU.subtract, ALU.mult)
                        last.then_inc(norm_dve, 1)
                for u in range(2):
                    dve.wait_ge(logits_done[u], NG // 2 * (f + 1))
                L, w, m, m2, gap, e2, choice = self.L, self.w, self.m, self.m2, self.gap, self.e2, self.choice
                bt = lambda a: a.unsqueeze(2).to_broadcast([P, NT, E])
                be = lambda a: a.unsqueeze(1).to_broadcast([P, NT, E])
                oh = [choice[:, :, k, :].rearrange("p e t -> p t e") for k in range(K)]
                ch.then(dve.tensor_copy(L[:], bank[2][:, 0:NT * E].rearrange("p (t e) -> p t e", e=E)))
                for k in range(K):
                    mk = m if k == 0 else m2
                    ch.then(dve.tensor_reduce(mk[:], L[:], AX, ALU.max))
                    ch.then(dve.tensor_tensor(w[:], L[:], bt(mk[:]), ALU.is_equal))
                    ch.then(dve.tensor_tensor(w[:], w[:], be(prefer[:]), ALU.mult))
                    ch.then(dve.tensor_reduce(self.top[:], w[:], AX, ALU.max))
                    ch.then(dve.tensor_tensor(oh[k], w[:], bt(self.top[:]), ALU.is_equal))
                    if k == 0:
                        ch.then(dve.scalar_tensor_tensor(L[:], oh[0], FAR, L[:], ALU.mult, ALU.add))
                dve.tensor_tensor(gap[:], m2[:], m[:], ALU.subtract).then_inc(gap_done, 1)
                dve.tensor_copy(self.top[:, 0:1], m[:, 0:1]).then_inc(onehot_done, 1)
                ek = lambda a: a.unsqueeze(2).to_broadcast([P, E, K * NT])
                ch2 = choice[:].rearrange("p e k t -> p e (k t)")
                by_tok = lambda a: a.rearrange("p e j -> p j e")
                ch.then(dve.tensor_tensor(self.pos[:], ch2, ek(expert_base[:]), ALU.mult))
                ch.then(dve.tensor_reduce(self.base[:], by_tok(self.pos[:]), AX, ALU.add))
                dve.wait_ge(counts_done, f + 1)
                fl = lambda a: a.rearrange("p e j -> p (e j)")
                ch.then(dve.tensor_tensor_scan(fl(self.cum[:]), fl(carry[:]), bank[4][:], 0.0, ALU.mult, ALU.add))
                ch.then(dve.tensor_tensor(fl(self.cum[:]), fl(self.cum[:]), bank[4][:], ALU.subtract))
                ch.then(dve.scalar_tensor_tensor(fl(self.cum[:]), bank[3][:], -1.0, fl(self.cum[:]), ALU.add, ALU.add))
                ch.then(dve.tensor_tensor(self.pos[:], self.cum[:], ch2, ALU.mult))
                ch.then(dve.tensor_reduce(self.at[:], by_tok(self.pos[:]), AX, ALU.add))
                ch.add(dve.tensor_copy(self.at_i[:], self.at[:]))
                ch.then(dve.tensor_scalar(self.valid[:], self.at[:], float(CAP), None, ALU.is_lt))
                ch.add(dve.tensor_scalar(self.at_i[:], self.at_i[:], P - 1, None, ALU.bitwise_and))
                ch.then(dve.tensor_tensor(self.slotf[:], self.at[:], self.valid[:], ALU.mult))
                ch.add(dve.tensor_copy(self.lof[:], self.at_i[:]))
                ch.then(dve.tensor_tensor(slot[:].rearrange("p k t -> p (k t)"), self.slotf[:], self.base[:], ALU.add))
                ch.then(dve.tensor_tensor(self.hif[:], self.at[:], self.lof[:], ALU.subtract))
                ch.then(dve.tensor_tensor(self.hi_oh[:], self.hif[:].unsqueeze(2).to_broadcast([P, K * NT, NCH]),
                                          iota_hi[:].unsqueeze(1).to_broadcast([P, K * NT, NCH]), ALU.is_equal))
                for k in range(K):
                    ch.add(dve.tensor_tensor(self.hi_oh[:, k * NT:(k + 1) * NT], self.hi_oh[:, k * NT:(k + 1) * NT],
                                             token_id[:].unsqueeze(2).to_broadcast([P, NT, NCH]), ALU.mult))
                ch.wait()
                for q in range(4):
                    js = slice(q * 16, q * 16 + 16)
                    for e in range(E):
                        pass
                    ch.add(dve.tensor_tensor(self.hi_tok[:, js].rearrange("p j (e h) -> p j e h", e=E),
                                             ch2[:, :, js].rearrange("p e j -> p j e").unsqueeze(3).to_broadcast([P, 16, E, NCH]),
                                             self.hi_oh[:, js].unsqueeze(2).to_broadcast([P, 16, E, NCH]), ALU.mult))
                    ch.wait()
                    for j in range(q * 16, q * 16 + 16):
                        if K * NT * f + j >= 8:
                            dve.wait_ge(lo_used, K * NT * f + j - 7)
                        dve.tensor_scalar(self.lo[:, j % 8], iota_lo[:], self.lof[:, j:j + 1], None, ALU.is_equal).then_inc(lo_ready, 1)
                dve.wait_ge(exp_gap, f + 1)
                gf = lambda k: gate[:, k]
                ch.then(dve.tensor_scalar(self.top[:], e2[:], 1.0, None, ALU.add))
                ch.then(dve.reciprocal(gap[:], self.top[:]))
                vk = lambda k: self.valid[:, k * NT:(k + 1) * NT]
                ch.add(dve.scalar_tensor_tensor(gf(0), gap[:], 0.5, vk(0), ALU.mult, ALU.mult))
                ch.then(dve.tensor_tensor(e2[:], e2[:], gap[:], ALU.mult))
                ch.then(dve.scalar_tensor_tensor(gf(1), e2[:], 0.5, vk(1), ALU.mult, ALU.mult))
                dve.wait_ge(lo_used, K * NT * (f + 1))
                ch.then(dve.tensor_copy(gidx[:], bank[5][:, 0:E * NCH]))

        class Experts:

            def __init__(self, f, stage):
                self.f, self.b = f, NSB * f
                new = lambda name, shape, dt=F32: scoped(stage, f"{name}_{f}", shape, dt)
                self.xg = new("xg", [P, 4, GT, C])
                self.xh = new("xh", [P, 2, 512], F32R)
                self.xl = new("xl", [P, 2, 512], F32R)
                self.hf = new("hf", [P, HC, 512])
                self.hh = new("hh", [P, 2, HC, 512], F32R)
                self.hl = new("hl", [P, 2, HC, 512], F32R)
                self.yT = new("yT", [P, 512])
                self.y_sb = new("y_sb", [P, 2, GT, C])

            def schedule(self, eng, step, warm=2):
                step(0, 0)
                step(0, 1)
                with eng.Fori(0, 3) as i:
                    for r in range(2, 6):
                        step(i, r)
                for r in range(2, 6):
                    step(3, r)

            @staticmethod
            def has(i, r, d):
                if isinstance(i, int):
                    return 0 <= 4 * i + r - d < NSB
                return True

            def sync(self, sp):
                def step(i, r):
                    s = 4 * i + r
                    if self.has(i, r, 2):
                        sp.wait_ge(y_ready, self.b + s - 1)
                        sp.dma_start(rows(y_dram, (s - 2) * 512), self.y_sb[:, r % 2]).then_inc(y_stored[r % 2], 16)
                    if r % 2 == 0 and not (isinstance(i, int) and (s < 2 or s + 2 >= NSB)):
                        slot_ = (r // 2 + 1) % 2
                        sp.wait_ge(hl_free, self.b + s)
                        sp.dma_start(wst[slot_][:].bitcast(F32), wres[:, bass.ds(2 * i + r // 2 + 1, 1)].rearrange("p a w n -> p (a w) n").bitcast(F32)).then_inc(w_loaded[slot_], 16)
                        sp.wait_ge(yT_ready, self.b + s)
                        sp.dma_start(bst[slot_][:], bcol[:, bass.ds((2 * i + r // 2 + 1) * (HC + 1), HC + 1)]).then_inc(w_loaded[slot_], 16)
                self.schedule(sp, step)
                for u in range(2):
                    sp.wait_ge(y_stored[u], 16 * NSB // 2 * (self.f + 1))

            def gpsimd(self, gp):
                for s in range(NSB):
                    S = self.b + s
                    if S >= 4:
                        gp.wait_ge(xT_ready, S - 3)
                    for t in range(GT):
                        j = GT * s + t
                        gp.indirect_dma_start(out=self.xg[:, s % 4, t], out_offset=None, in_=xn_dram,
                                              in_offset=bass.IndirectOffsetOnAxis(ap=gidx[:, j:j + 1], axis=0)).then_inc(gathered[s % 4], 16)

            def tensor(self, pe):
                f, b = self.f, self.b

                def turn(i, r):
                    pe.wait_ge(gathered[r % 4], 64 * (4 * f + i + r // 4 + 1))
                    pe.wait_ge(xl_ready, b + 4 * i + r)
                    for t in range(GT):
                        last = nc.tensor.transpose(bank[0][:, t * P:(t + 1) * P], self.xg[:, r % 4, t], ident[:])
                    last.then_inc(xT_ready, 1)

                def up(i, r, c):
                    w = wst[(r // 2) % 2]
                    s = 4 * i + r
                    if c == 0:
                        pe.wait_ge(xl_ready, b + s + 1)
                        pe.wait_ge(w_loaded[(r // 2) % 2], 32 * (4 * f + i + r // 4 + 1))
                    pe.wait_ge(hf_ready[c], b + s)
                    at = slice(c * P, (c + 1) * P)
                    nc.tensor.matmul(bank[1 + c][:], w[:, 0, at], self.xh[:, r % 2], start=True, stop=False)
                    nc.tensor.matmul(bank[1 + c][:], w[:, 0, at], self.xl[:, r % 2], start=False, stop=False)
                    nc.tensor.matmul(bank[1 + c][:], w[:, 2, at], self.xh[:, r % 2], start=False, stop=True).then_inc(h_ready[c], 1)

                def down(i, r, c):
                    w = wst[(r // 2) % 2]
                    s = 4 * i + r
                    pe.wait_ge(hl_ready[c], b + s + 1)
                    if c == 0:
                        pe.wait_ge(yT_ready, b + s)
                    at = slice(c * P, (c + 1) * P)
                    nc.tensor.matmul(bank[5][:], w[:, 1, at], self.hh[:, r % 2, c], start=(c == 0), stop=False)
                    nc.tensor.matmul(bank[5][:], w[:, 1, at], self.hl[:, r % 2, c], start=False, stop=False)
                    last = nc.tensor.matmul(bank[5][:], w[:, 3, at], self.hh[:, r % 2, c], start=False, stop=(c == HC - 1))
                    if c == HC - 1:
                        last.then_inc(hl_free, 1)

                def back(i, r):
                    s = 4 * i + r
                    pe.wait_ge(yT_ready, b + s + 1)
                    pe.wait_ge(y_ready, b + s)
                    for t in range(GT):
                        last = nc.tensor.transpose(bank[6][:, t * P:(t + 1) * P], self.yT[:, t * P:(t + 1) * P], ident[:])
                    last.then_inc(ytr_ready, 1)

                def step(i, r):
                    for c in range(HC):
                        if self.has(i, r, 0):
                            up(i, r, c)
                        if c == 0 and self.has(i, r, 2):
                            back(i, r - 2)
                        if self.has(i, r, 1):
                            down(i, r - 1, c)
                        if c == 0 and self.has(i, r, -1):
                            turn(i, r + 1)
                turn(0, 0)
                self.schedule(pe, step)

            def scalar(self, act):
                f, b = self.f, self.b

                def high(i, r):
                    act.wait_ge(xT_ready, b + 4 * i + r + 1)
                    nc.scalar.copy(self.xh[:, r % 2], bank[0][:]).then_inc(xh_ready, 1)

                def step(i, r):
                    s = 4 * i + r
                    if self.has(i, r, 2):
                        act.wait_ge(hl_free, b + s - 1)
                        act.wait_ge(ytr_ready, b + s - 2)
                        nc.scalar.activation(self.yT[:], bank[5][:], ACT.Identity,
                                             bias=bst[(r // 2 + 1) % 2][:, HC:HC + 1]).then_inc(yT_ready, 1)
                    for c in range(HC):
                        if self.has(i, r, 0):
                            act.wait_ge(h_ready[c], b + s + 1)
                            act.wait_ge(hl_ready[c], b + s)
                            bias = bst[(r // 2) % 2][:, c:c + 1]
                            one = nc.scalar.activation(self.hf[:, c], bank[1 + c][:], ACT.Relu, bias=bias)
                            if c == HC - 1:
                                one = nc.scalar.activation(self.hh[:, r % 2, c], bank[1 + c][:], ACT.Relu, bias=bias)
                            one.then_inc(hf_ready[c], 1)
                        if c == 0 and self.has(i, r, -1):
                            high(i, r + 1)
                high(0, 0)
                self.schedule(act, step)

            def vector(self, dve):
                f, b = self.f, self.b

                def low(i, r):
                    dve.wait_ge(xh_ready, b + 4 * i + r + 1)
                    dve.tensor_tensor(self.xl[:, r % 2], bank[0][:], self.xh[:, r % 2].bitcast(F32), ALU.subtract).then_inc(xl_ready, 1)

                def step(i, r):
                    s = 4 * i + r
                    here = self.has(i, r, 0)

                    def h_high(c):
                        dve.wait_ge(hf_ready[c], b + s + 1)
                        dve.tensor_copy(self.hh[:, r % 2, c], self.hf[:, c]).then_inc(hh_ready[c], 1)

                    def h_low(c):
                        if c < HC - 1:
                            dve.wait_ge(hh_ready[c], b + s + 1)
                        else:
                            dve.wait_ge(hf_ready[c], b + s + 1)
                        dve.tensor_tensor(self.hl[:, r % 2, c], self.hf[:, c], self.hh[:, r % 2, c].bitcast(F32), ALU.subtract).then_inc(hl_ready[c], 1)
                    if here:
                        h_high(0)
                    if self.has(i, r, 2):
                        u = r % 2
                        dve.wait_ge(ytr_ready, b + s - 1)
                        dve.wait_ge(y_stored[u], 16 * (8 * f + 2 * i + (r - 2) // 2))
                        dve.tensor_copy(self.y_sb[:, u].rearrange("p t c -> p (t c)"), bank[6][:]).then_inc(y_ready, 1)
                    if here:
                        h_low(0)
                    if self.has(i, r, -1):
                        low(i, r + 1)
                    if here:
                        h_high(1)
                        h_high(2) if False else None
                        h_low(1)
                        h_high(2)
                        h_low(2)
                        h_low(3)
                low(0, 0)
                self.schedule(dve, step)

        hl_free = sem("hl_free")

        ones_col = sem("ones_col")
        a_x1 = sem("a_x1")
        a_norm = sem("a_norm")
        a_turned = sem("a_turned")
        a_anT = sem("a_anT")
        a_q = sem("a_q")
        a_qact = sem("a_qact")
        a_qT = sem("a_qT")
        a_k = sem("a_k")
        a_kact = sem("a_kact")
        a_vact = sem("a_vact")
        a_kk = sem("a_kk")
        a_kv = sem("a_kv")
        a_kvs = sem("a_kvs")
        a_num = sem("a_num")
        a_at = sem("a_at")
        a_att = sem("a_att")
        a_atT = sem("a_atT")
        a_o = sem("a_o")
        a_x2 = sem("a_x2")

        class Attention:

            def __init__(self, stage, f):
                self.f = f
                new = lambda name, shape: scoped(stage, f"{name}_{f}", shape)
                self.yg = new("yg", [P, 2, K, GT, C])
                self.x1 = new("x1", [P, 2, GT, C])
                if f == 1:
                    return
                self.an = new("an", [P, 2, GT, C])
                self.anT = new("anT", [P, 2, SEQ])
                self.ex = new("ex", [P, 2, SEQ])
                self.re_ = new("re", [P, 2, SEQ])
                self.qT = new("qT", [P, 2, SEQ])
                self.kk = new("kk", [P, 2, GT, C])
                self.vv = new("vv", [P, 2, GT, C + 1])
                self.kv = new("kv", [P, 2, C + HEADS])
                self.den = new("den", [P, 2, GT, HEADS])
                self.atT = new("atT", [P, 2, SEQ])
                self.sta = new("sta", [P, 2 * GT, 6])
                self.mean = new("mean_a", [P, 2 * GT])
                self.nwa = new("nwa", [P, 5, 2 * GT])
                self.rsa = new("rsa", [P, 2, 2 * GT])

            def gather(self, gp):
                f = self.f
                for n in range(NG):
                    u = n % 2
                    if f * NG + n >= 2:
                        gp.wait_ge(yg_used[u], (NG * f + n) // 2)
                    for k in range(K):
                        for t in range(GT):
                            gp.indirect_dma_start(out=self.yg[:, u, k, t], out_offset=None, in_=y_dram,
                                                  in_offset=bass.IndirectOffsetOnAxis(ap=slot[:, k, GT * n + t:GT * n + t + 1], axis=0)).then_inc(yg_in[u], 16)

            def tensor(self, pe):
                def turn(u, n, i):
                    pe.wait_ge(a_norm, n + 1)
                    pe.wait_ge(a_anT, n)
                    for t in range(GT):
                        last = nc.tensor.transpose(bank[0][:, t * P:(t + 1) * P], self.an[:, u, t], ident[:])
                    last.then_inc(a_turned, 1)

                def qkv(u, n, i):
                    pe.wait_ge(a_anT, n + 1)
                    pe.wait_ge(a_qact, n)
                    pe.wait_ge(a_x2, 2 * i)
                    nc.tensor.matmul(bank[1][:], WT[:, 0], self.anT[:, u], start=True, stop=True).then_inc(a_q, 1)
                    pe.wait_ge(a_kact, n)
                    pe.wait_ge(a_vact, n)
                    for w in (0, 1):
                        for t in range(GT):
                            at = slice(t * P, (t + 1) * P)
                            nc.tensor.matmul(bank[2 + w][:, at], self.anT[:, u, at], WT[:, 1 + w], start=True, stop=False)
                            last = nc.tensor.matmul(bank[2 + w][:, at], ones2[:], bpair[:, w], start=False, stop=True)
                    last.then_inc(a_k, 1)

                def keysum(u, n, i):
                    pe.wait_ge(a_kk, n + 1)
                    pe.wait_ge(ones_col, 1)
                    pe.wait_ge(a_vact, n + 1)
                    pe.wait_ge(a_kvs, n)
                    for t in range(GT):
                        last = nc.tensor.matmul(bank[4][:, 0:C + 1], self.kk[:, u, t], self.vv[:, u, t], start=(t == 0), stop=(t == GT - 1))
                    last.then_inc(a_kv, 1)

                def query(u, n, i):
                    pe.wait_ge(a_kvs, n + 1)
                    pe.wait_ge(a_qT, n + 1)
                    pe.wait_ge(a_at, n)
                    for t in range(GT):
                        at = slice(t * P, (t + 1) * P)
                        nc.tensor.matmul(bank[5][:, at], self.qT[:, u, at], self.kv[:, u, 0:C], start=True, stop=True)
                        last = nc.tensor.matmul(bank[6][:, t * HEADS:(t + 1) * HEADS], self.qT[:, u, at],
                                                self.kv[:, u, C:C + HEADS], start=True, stop=True)
                    last.then_inc(a_num, 1)

                def turn_out(u, n, i):
                    pe.wait_ge(a_at, n + 1)
                    pe.wait_ge(a_atT, n)
                    for t in range(GT):
                        last = nc.tensor.transpose(bank[7][:, t * P:(t + 1) * P], self.an[:, u, t], ident[:])
                    last.then_inc(a_att, 1)

                def project(u, n, i):
                    pe.wait_ge(a_atT, n + 1)
                    pe.wait_ge(a_x2, n)
                    pe.wait_ge(a_qact, 2 * i + 2)
                    for t in range(GT):
                        at = slice(t * P, (t + 1) * P)
                        nc.tensor.matmul(bank[1][:, at], self.atT[:, u, at], WT[:, 3], start=True, stop=False)
                        last = nc.tensor.matmul(bank[1][:, at], ones2[:], bpair[:, 2], start=False, stop=True)
                    last.then_inc(a_o, 1)

                with pe.Fori(0, NG // 2) as i:
                    for part in (turn, qkv, keysum, query, turn_out, project):
                        for u in range(2):
                            part(u, 2 * i + u, i)

            def scalar(self, act, ch):
                def norm(u, n, i):
                    act.wait_ge(a_x1, i + 1)
                    for t in range(GT):
                        q = GT * u + t
                        last = nc.scalar.activation(self.an[:, u, t], self.x1[:, u, t], ACT.Identity,
                                                    bias=self.rsa[:, 1, q:q + 1], scale=self.rsa[:, 0, q:q + 1])
                    last.then_inc(a_norm, 1)

                def anT_out(u, n, i):
                    act.wait_ge(a_turned, n + 1)
                    nc.scalar.copy(self.anT[:, u], bank[0][:]).then_inc(a_anT, 1)

                def q_act(u, n, i):
                    act.wait_ge(a_q, n + 1)
                    bias = bcol[:, NBIAS - 1:NBIAS]
                    ch.add(nc.scalar.activation(self.ex[:, u], bank[1][:], ACT.Relu, bias=nbq[:], scale=-1.0))
                    nc.scalar.activation(self.re_[:, u], bank[1][:], ACT.Relu, bias=bias)
                    ch.wait()
                    nc.scalar.activation(self.ex[:, u], self.ex[:, u], ACT.Exp, scale=-1.0).then_inc(a_qact, 1)

                def k_act(u, n, i):
                    act.wait_ge(a_k, n + 1)
                    act.wait_ge(a_qT, n + 1)
                    ch.add(nc.scalar.activation(self.ex[:, u], bank[2][:], ACT.Relu, scale=-1.0))
                    nc.scalar.activation(self.re_[:, u], bank[2][:], ACT.Relu)
                    ch.wait()
                    nc.scalar.activation(self.ex[:, u], self.ex[:, u], ACT.Exp, scale=-1.0).then_inc(a_kact, 1)
                    nc.scalar.copy(self.vv[:, u, :, 0:C], bank[3][:].rearrange("p (t c) -> p t c", c=C)).then_inc(a_vact, 1)

                def atT_out(u, n, i):
                    act.wait_ge(a_att, n + 1)
                    nc.scalar.copy(self.atT[:, u], bank[7][:]).then_inc(a_atT, 1)

                with act.Fori(0, NG // 2) as i:
                    ch.enter(i, 4)
                    for part in (norm, anT_out, q_act, k_act, atT_out):
                        for u in range(2):
                            part(u, 2 * i + u, i)
                ch.leave(NG // 2)

            def front(self, dve, ch, i):
                for u in range(2):
                    n = 2 * i + u
                    dve.wait_ge(yg_in[u], 128 * (i + 1))
                    for t in range(GT):
                        tt = GT * n + t
                        xt = x_sb[:, bass.ds(tt, 1), :].rearrange("p a c -> p (a c)")
                        ch.add(dve.scalar_tensor_tensor(self.x1[:, u, t], self.yg[:, u, 0, t], gate[:, 0, bass.ds(tt, 1)], xt, ALU.mult, ALU.add))
                    ch.wait()
                    for t in range(GT):
                        tt = GT * n + t
                        ch.add(dve.scalar_tensor_tensor(self.x1[:, u, t], self.yg[:, u, 1, t], gate[:, 1, bass.ds(tt, 1)], self.x1[:, u, t], ALU.mult, ALU.add))
                    dve.tensor_copy(self.nwa[:, 4, 0:1], self.yg[:, u, 1, GT - 1, 0:1]).then_inc(yg_used[u], 1)
                ch.wait()
                for u in range(2):
                    for t in range(GT):
                        ch.add(dve.bn_stats(self.sta[:, GT * u + t], self.x1[:, u, t]))
                ch.wait()
                layer_norm_scalars(ch, dve, self.sta, self.mean[:], self.rsa[:, 0], self.rsa[:, 1], [self.nwa[:, q] for q in range(4)])
                dve.tensor_copy(self.nwa[:, 4, 0:1], self.mean[:, 0:1]).then_inc(a_x1, 1)

            FRONT = 16 + 8 + 7 + 3 + 9 + 1

            def vector(self, dve, ch):
                def q_sum(u, n, i):
                    dve.wait_ge(a_qact, n + 1)
                    dve.tensor_tensor(self.qT[:, u], self.ex[:, u], self.re_[:, u], ALU.add).then_inc(a_qT, 1)

                def k_sum(u, n, i):
                    dve.wait_ge(a_kact, n + 1)
                    dve.tensor_tensor(self.kk[:, u].rearrange("p t c -> p (t c)"), self.ex[:, u], self.re_[:, u], ALU.add).then_inc(a_kk, 1)

                def kv_mask(u, n, i):
                    dve.wait_ge(a_kv, n + 1)
                    ch.add(dve.tensor_tensor(self.kv[:, u, 0:C], bank[4][:, 0:C], block_mask[:], ALU.mult))
                    ch.add(dve.tensor_tensor(self.kv[:, u, C:C + HEADS], head_mask[:], bank[4][:, C:C + 1].to_broadcast([P, HEADS]), ALU.mult))
                    ch.wait()
                    dve.tensor_copy(self.nwa[:, 4, 1:2], self.kv[:, u, 0:1]).then_inc(a_kvs, 1)

                def divide(u, n, i):
                    dve.wait_ge(a_num, n + 1)
                    ch.then(dve.tensor_scalar(self.den[:, u], bank[6][:, 0:GT * HEADS].rearrange("p (t h) -> p t h", h=HEADS), 1e-6, None, ALU.max))
                    ch.then(dve.reciprocal(self.den[:, u], self.den[:, u]))
                    dve.tensor_tensor(self.an[:, u].rearrange("p t (h d) -> p (t h) d", d=HD), bank[5][:].rearrange("p (a d) -> p a d", d=HD),
                                      self.den[:, u].rearrange("p t h -> p (t h)").unsqueeze(2).to_broadcast([P, GT * HEADS, HD]), ALU.mult).then_inc(a_at, 1)

                def residual(u, n, i):
                    dve.wait_ge(a_o, n + 1)
                    ch.add(dve.tensor_tensor(x_sb[:, bass.ds(GT * n, GT), :], bank[1][:].rearrange("p (t c) -> p t c", c=C), self.x1[:, u], ALU.add))
                    ch.wait()
                    dve.tensor_copy(self.nwa[:, 4, 2:3], self.x1[:, u, 0, 0:1]).then_inc(a_x2, 1)
                    for t in range(GT):
                        at = bass.ds(GT * n + t, 1)
                        ch.add(dve.bn_stats(stats[:, at].rearrange("p a s -> p (a s)"), x_sb[:, at].rearrange("p a c -> p (a c)")))

                with dve.Fori(0, NG // 2) as i:
                    ch.enter(i, self.FRONT + 2 * (2 + 2 + 1 + 4))
                    self.front(dve, ch, i)
                    for part in (q_sum, k_sum, kv_mask, divide, residual):
                        for u in range(2):
                            part(u, 2 * i + u, i)
                    ch.wait()
                ch.leave(NG // 2)

        chain = [None]

        def dve_chain(dve):
            if chain[0] is None:
                chain[0] = Chain(dve, dve_step)
            chain[0].eng = dve
            return chain[0]

        with ExitStack() as stage, nc.Block() as block:
            route = Route(0, stage)
            wexp_raw = scoped(stage, "wexp_raw", [P, 2, 2, H])
            wraw = scoped(stage, "wraw", [P, 4, C])
            brows = scoped(stage, "brows", [NBIAS, P])

            @block.sync
            def _(sp):
                with sp.Fori(0, NG // 2) as i:
                    for u in range(2):
                        sp.wait_ge(x_arrived[u], 16 * i)
                        sp.dma_start(x_sb[:, bass.ds((2 * i + u) * GT, GT), :], rows(xf, (2 * i + u) * SEQ)).then_inc(x_arrived[u], 16)
                with sp.Fori(0, E // 2) as i:
                    for u in range(2):
                        e = 2 * i + u
                        sp.wait_ge(exp_lo, 2 * i)
                        sp.dma_start(wexp_raw[:, u, 0], w1[bass.ds(e, 1)].rearrange("a m h -> m (a h)")).then_inc(exp_raw_in[u], 16)
                        sp.dma_start(wexp_raw[:, u, 1].rearrange("p (c m) -> p c m", m=C),
                                     w2[bass.ds(e, 1)].rearrange("a (c p) m -> p (a c) m", p=P)).then_inc(exp_raw_in[u], 16)
                route.sync(sp)

            @block.gpsimd
            def _(gp):
                ch = Chain(gp, const_chain)
                ch.add(nc.gpsimd.memset(ident[:], 0.0))
                ch.add(nc.gpsimd.memset(tri[:], 1.0))
                ch.add(nc.gpsimd.memset(head_mask[:], 1.0))
                ch.add(nc.gpsimd.memset(ones_row[:], 1.0))
                ch.add(nc.gpsimd.memset(part01[:], 0.0))
                ch.add(nc.gpsimd.memset(ones_bf[:], 1.0))
                ch.then(nc.gpsimd.memset(carry[:], 1.0))
                fl = dict(allow_small_or_imprecise_dtypes=True)
                ch.add(nc.gpsimd.affine_select(out=ident[:], in_=ident[:], compare_op=ALU.not_equal, fill=1.0, base=0, pattern=[[-1, P]], channel_multiplier=1))
                ch.add(nc.gpsimd.affine_select(out=tri[:], in_=tri[:], compare_op=ALU.is_ge, fill=0.0, base=0, pattern=[[1, P]], channel_multiplier=-1))
                ch.add(nc.gpsimd.affine_select(out=part01[:], in_=part01[:], compare_op=ALU.not_equal, fill=1.0, base=0, pattern=[[-1, 2]], channel_multiplier=1))
                ch.add(nc.gpsimd.memset(carry[:, :, 0:1], 0.0))
                ch.then(nc.gpsimd.affine_select(out=head_mask[:], in_=head_mask[:], compare_op=ALU.is_ge, fill=0.0, base=0, pattern=[[-HD, HEADS]], channel_multiplier=1))
                ch.then(nc.gpsimd.affine_select(out=head_mask[:], in_=head_mask[:], compare_op=ALU.is_ge, fill=0.0, base=HD - 1, pattern=[[HD, HEADS]], channel_multiplier=-1))
                ch.add(nc.gpsimd.tensor_copy(block_mask[:].rearrange("p (h d) -> p h d", d=HD), head_mask[:].unsqueeze(2).to_broadcast([P, HEADS, HD])))
                ch.add(nc.gpsimd.iota(iota_lo[:], pattern=[[1, P]], base=0, channel_multiplier=0, **fl))
                ch.add(nc.gpsimd.iota(prefer[:], pattern=[[-1, E]], base=E, channel_multiplier=0, **fl))
                ch.add(nc.gpsimd.iota(iota_hi[:], pattern=[[P, NCH]], base=0, channel_multiplier=0, **fl))
                ch.add(nc.gpsimd.iota(expert_base[:], pattern=[[CAP, E]], base=0, channel_multiplier=0, **fl))
                ch.then(nc.gpsimd.iota(token_id[:], pattern=[[P, NT]], base=0, channel_multiplier=1, **fl))
                nc.gpsimd.tensor_copy(ones2[:], ones_row[:]).then_inc(consts, 1)
                with gp.Fori(0, E // 2) as i:
                    for u in range(2):
                        gp.wait_ge(exp_hi, 2 * i + u + 1)
                        w = wres[:, bass.ds(2 * i + u, 1)].rearrange("p a w n -> p (a w) n")
                        nc.gpsimd.tensor_tensor(w[:, 2:4], wexp_raw[:, u], w[:, 0:2].bitcast(F32), ALU.subtract).then_inc(exp_lo, 1)

            @block.scalar
            def _(act):
                for j, W in enumerate((Wq, Wk, Wv, Wo)):
                    act.dma_start(wraw[:, j], W).then_inc(small_in[0], 16)
                act.dma_start(wg_sb[:], wg).then_inc(small_in[2], 16)
                act.dma_start(brows[0:E * HC], b1.rearrange("e (c p) -> (e c) p", p=P)).then_inc(small_in[1], 16)
                act.dma_start(brows[E * HC:E * HC + E], b2).then_inc(small_in[1], 16)
                act.dma_start(brows[NBIAS - 1:NBIAS], bq.rearrange("(a n) -> a n", a=1)).then_inc(small_in[1], 16)
                for j, bias in enumerate((bk, bv, bo)):
                    for row in range(2):
                        act.dma_start(brow[row:row + 1, j], bias.rearrange("(a n) -> a n", a=1)).then_inc(small_in[1], 16)
                act.wait_ge(WT_ps, 1)
                nc.scalar.copy(WT[:].rearrange("p w c -> p (w c)"), bank[6][:]).then_inc(WT_sb, 1)
                by_expert = bcol[:, 0:E * (HC + 1)].rearrange("p (e c) -> p e c", c=HC + 1)
                nc.scalar.copy(by_expert[:, :, 0:HC], bank[7][:, 0:E * HC].rearrange("p (e c) -> p e c", c=HC))
                nc.scalar.copy(by_expert[:, :, HC], bank[7][:, E * HC:E * HC + E])
                nc.scalar.copy(bcol[:, NBIAS - 1:NBIAS], bank[7][:, NBIAS - 1:NBIAS])
                nc.scalar.mul(nbq[:], bank[7][:, NBIAS - 1:NBIAS], -1.0).then_inc(WT_sb, 1)
                with act.Fori(0, E // 2) as i:
                    for u in range(2):
                        act.wait_ge(exp_raw_in[u], 32 * (i + 1))
                        w = wres[:, bass.ds(2 * i + u, 1)].rearrange("p a w n -> p (a w) n")
                        nc.scalar.copy(w[:, 0:2], wexp_raw[:, u]).then_inc(exp_hi, 1)
                route.scalar(act)

            @block.tensor
            def _(pe):
                pe.wait_ge(consts, 1)
                pe.wait_ge(small_in[0], 64)
                for j in range(4):
                    nc.tensor.transpose(bank[6][:, j * P:(j + 1) * P], wraw[:, j], ident[:])
                pe.wait_ge(small_in[1], 16 * 9)
                nc.tensor.transpose(bank[7][:, 0:NBIAS], brows[:], ident[0:NBIAS, 0:NBIAS]).then_inc(WT_ps, 1)
                pe.wait_ge(small_in[2], 16)
                route.tensor(pe)

            @block.vector
            def _(dve):
                ch = dve_chain(dve)
                with dve.Fori(0, NG // 2) as i:
                    ch.enter(i, 2 * GT)
                    for u in range(2):
                        g = 2 * i + u
                        dve.wait_ge(x_arrived[u], 16 * (i + 1))
                        for t in range(GT):
                            at = bass.ds(GT * g + t, 1)
                            ch.add(dve.bn_stats(stats[:, at].rearrange("p a s -> p (a s)"), x_sb[:, at].rearrange("p a c -> p (a c)")))
                ch.leave(NG // 2)
                ch.wait()
                dve.wait_ge(consts, 1)
                dve.wait_ge(small_in[1], 16 * 9)
                ch.then(dve.tensor_copy(bhi[:], brow[:]))
                ch.add(dve.tensor_tensor(blo[:], brow[:], bhi[:].bitcast(F32), ALU.subtract))
                ch.then(dve.tensor_scalar(bsum[:], bhi[:].bitcast(F32), part01[:, 0:1], None, ALU.mult))
                ch.then(dve.scalar_tensor_tensor(bpair[:], blo[:].bitcast(F32), part01[:, 1:2], bsum[:], ALU.mult, ALU.add))
                route.vector(dve, ch)

        def experts_block(f):
            with ExitStack() as stage, nc.Block() as block:
                experts = Experts(f, stage)

                @block.sync
                def _(sp):
                    experts.sync(sp)

                @block.gpsimd
                def _(gp):
                    experts.gpsimd(gp)

                @block.tensor
                def _(pe):
                    experts.tensor(pe)

                @block.scalar
                def _(act):
                    experts.scalar(act)

                @block.vector
                def _(dve):
                    experts.vector(dve)

        experts_block(0)

        with ExitStack() as stage, nc.Block() as block:
            attention = Attention(stage, 0)

            @block.gpsimd
            def _(gp):
                nc.gpsimd.memset(attention.vv[:, :, :, C:C + 1], 1.0).then_inc(ones_col, 1)
                attention.gather(gp)

            @block.tensor
            def _(pe):
                attention.tensor(pe)

            @block.scalar
            def _(act):
                attention.scalar(act, Chain(act, act_step))

            @block.vector
            def _(dve):
                attention.vector(dve, dve_chain(dve))

        with ExitStack() as stage, nc.Block() as block:
            route = Route(1, stage)

            @block.sync
            def _(sp):
                route.sync(sp)

            @block.scalar
            def _(act):
                route.scalar(act)

            @block.tensor
            def _(pe):
                route.tensor(pe)

            @block.vector
            def _(dve):
                route.vector(dve, dve_chain(dve))

        experts_block(1)

        with ExitStack() as stage, nc.Block() as block:
            last_sum = Attention(stage, 1)

            @block.gpsimd
            def _(gp):
                last_sum.gather(gp)

            @block.vector
            def _(dve):
                ch = dve_chain(dve)
                with dve.Fori(0, NG // 2) as i:
                    ch.enter(i, 2 * GT)
                    for u in range(2):
                        n = 2 * i + u
                        dve.wait_ge(yg_in[u], 128 * (NG // 2 + i + 1))
                        dve.wait_ge(out_stored[u], 16 * i)
                        for t in range(GT):
                            tt = GT * n + t
                            xt = x_sb[:, bass.ds(tt, 1), :].rearrange("p a c -> p (a c)")
                            ch.add(dve.scalar_tensor_tensor(last_sum.x1[:, u, t], last_sum.yg[:, u, 0, t], gate[:, 0, bass.ds(tt, 1)], xt, ALU.mult, ALU.add))
                        ch.wait()
                        for t in range(GT):
                            tt = GT * n + t
                            last = dve.scalar_tensor_tensor(last_sum.x1[:, u, t], last_sum.yg[:, u, 1, t], gate[:, 1, bass.ds(tt, 1)], last_sum.x1[:, u, t], ALU.mult, ALU.add)
                        last.then_inc(yg_used[u], 1)
                ch.leave(NG // 2)

            @block.sync
            def _(sp):
                with sp.Fori(0, NG // 2) as i:
                    for u in range(2):
                        sp.wait_ge(yg_used[u], NG // 2 + i + 1)
                        sp.dma_start(rows(of, (2 * i + u) * SEQ), last_sum.x1[:, u]).then_inc(out_stored[u], 16)
                for u in range(2):
                    sp.wait_ge(out_stored[u], 16 * NG // 2)


_INS = ["L0_attn_x", "L0_attn_Wq", "L0_attn_bq", "L0_attn_Wk", "L0_attn_bk", "L0_attn_Wv", "L0_attn_bv", "L0_attn_Wo",
        "L0_attn_bo", "L0_ffn_wg", "L0_ffn_w1", "L0_ffn_b1", "L0_ffn_w2", "L0_ffn_b2"]
_OUTS = [((8, 512, 128), "float32")]


def kernel(**inputs):
    import numpy as _np
    import concourse.bacc as _bacc
    from concourse import mybir as _mybir
    from concourse.bass_utils import run_bass_kernel_spmd as _run

    nc = _bacc.Bacc("TRN2", target_bir_lowering=False, num_devices=1)
    arrays, args = {}, []
    for name in _INS:
        a = _np.ascontiguousarray(inputs[name])
        arrays[f"in_{name}"] = a
        args.append(nc.dram_tensor(f"in_{name}", a.shape, _mybir.dt.from_np(a.dtype), kind="ExternalInput").ap())
    for i, (shape, dtype) in enumerate(_OUTS):
        args.append(nc.dram_tensor(f"out_{i}", shape, _mybir.dt.from_np(_np.dtype(dtype)), kind="ExternalOutput").ap())
    macaron(nc, *args)
    r = _run(nc, [arrays], core_ids=[0])
    return r.results[0]["out_0"]
```

```python
import concourse.bass as bass
from concourse import mybir
from contextlib import ExitStack

F32 = mybir.dt.float32
F32R = mybir.dt.float32r
BF16 = mybir.dt.bfloat16
I32 = mybir.dt.int32
ALU = mybir.AluOpType
ACT = mybir.ActivationFunctionType
AX = mybir.AxisListType.X

P = 128
NB, SEQ, C = 8, 512, 128
N = NB * SEQ
NT = N // P
GT = SEQ // P
NG = NT // GT
E, K, H = 8, 2, 512
HC = H // P
LD = 12
XB = 4
RB = 4
CAP = K * N // E
NCH = CAP // P
NSB = E * CAP // 512
HEADS, HD = 16, 8
EPS = 1e-5
FAR = -3e38
RSQRT_SEED = 1597463007.0
NEG_EIGHTH_SEED = RSQRT_SEED - 3 * 2.0 ** 23 - 2.0 ** 31


class Chain:

    def __init__(self, eng, sem):
        self.eng, self.sem, self.n, self.turns = eng, sem, 0, 0

    def add(self, ins):
        ins.then_inc(self.sem, 1)
        self.n += 1

    def wait(self, n=None):
        self.eng.wait_ge(self.sem, self.turns + (self.n if n is None else n))

    def then(self, ins):
        self.add(ins)
        self.wait()

    def enter(self, i, count):
        self.start, self.count, self.turns = self.n, count, i * count

    def leave(self, turns):
        assert self.n - self.start == self.count, (self.n - self.start, self.count)
        self.n, self.turns = self.start + turns * self.count, 0


def macaron(nc, x_in, Wq, bq, Wk, bk, Wv, bv, Wo, bo, wg, w1, b1, w2, b2, out):
    ctx = ExitStack()
    with ctx:
        def sb(name, shape, dt=F32):
            return ctx.enter_context(nc.sbuf_tensor(name, shape, dt))

        def scoped(stage, name, shape, dt=F32):
            return stage.enter_context(nc.sbuf_tensor(name, shape, dt))

        def sem(name):
            return ctx.enter_context(nc.semaphore(name))

        def sems(name, n):
            return [sem(f"{name}{i}") for i in range(n)]

        xf = x_in.rearrange("b s c -> (b s) c")
        of = out.rearrange("b s c -> (b s) c")
        xn_dram = nc.dram_tensor("xn_dram", (N, C), F32, kind="Internal").ap()
        y_dram = nc.dram_tensor("y_dram", (E * CAP, C), F32, kind="Internal").ap()

        def rows(dram, at, tiles=GT):
            return dram[bass.ds(at, tiles * P), :].rearrange("(t p) c -> p t c", p=P)

        ident = sb("ident", [P, P])
        tri = sb("tri", [P, P], BF16)
        ones_bf = sb("ones_bf", [P, P], BF16)
        iota_lo = sb("iota_lo", [P, P])
        prefer = sb("prefer", [P, E])
        iota_hi = sb("iota_hi", [P, NCH])
        expert_base = sb("expert_base", [P, E])
        token_id = sb("token_id", [P, NT])
        carry = sb("carry", [P, E, K * NT])
        head_mask = sb("head_mask", [P, HEADS])
        block_mask = sb("block_mask", [P, P])
        ones_row = sb("ones_row", [2, P])
        ones2 = sb("ones2", [2, P], F32R)
        part01 = sb("part01", [2, 2])
        wg_sb = sb("wg_sb", [P, E])
        WT = sb("WT", [P, 4, C])
        bcol = sb("bcol", [P, E * (HC + 1) + 1])
        nbq = sb("nbq", [P, 1])
        brow = sb("brow", [2, 3, C])
        bhi = sb("bhi", [2, 3, C], F32R)
        blo = sb("blo", [2, 3, C], F32R)
        bsum = sb("bsum", [2, 3, C])
        bpair = sb("bpair", [2, 3, C], F32R)
        wres = sb("wres", [P, E, 4, H], F32R)
        bst = [sb(f"bst{i}", [P, HC + 1]) for i in range(2)]
        wst = [sb(f"wst{i}", [P, 4, H], F32R) for i in range(2)]
        x_sb = sb("x_sb", [P, NT, C])
        stats = sb("stats", [P, NT, 6])
        mean = sb("mean", [P, NT])
        nw = sb("nw", [P, 5, NT])
        rstd = sb("rstd", [P, NT])
        nmr = sb("nmr", [P, NT])
        gate = sb("gate", [P, K, NT])
        slot = sb("slot", [P, K, NT], I32)
        gidx = sb("gidx", [P, E * NCH], I32)

        bank = [ctx.enter_context(nc.psum_tensor(f"bank{i}", [P, 512], F32)) for i in range(8)]

        consts = sem("consts")
        const_chain = sem("const_chain")
        small_in = sems("small_in", 3)
        x_arrived = sems("x_arrived", 4)
        stats_done = sems("stats_done", 2)
        exp_raw_in = sems("exp_raw_in", E)
        exp_hi = sem("exp_hi")
        exp_lo = sem("exp_lo")
        WT_ps = sem("WT_ps")
        WT_sb = sem("WT_sb")
        bpair_done = sem("bpair_done")
        dve_step = sem("dve_step")
        act_step = sem("act_step")
        rstd_done = sem("rstd_done")
        norm_dve = sem("norm_dve")
        norm_act = sem("norm_act")
        turned = sem("turned")
        xnT_ready = sem("xnT_ready")
        logits_done = sem("logits_done")
        xn_stored = sems("xn_stored", XB)
        gap_done = sem("gap_done")
        exp_gap = sem("exp_gap")
        counts_done = sem("counts_done")
        lo_ready = sem("lo_ready")
        lo_act = sem("lo_act")
        hi_ready = sems("hi_ready", 2)
        slots_known = sem("slots_known")
        lo_used = sem("lo_used")
        tokens_copied = sem("tokens_copied")
        inverse_done = sem("inverse_done")
        gathered = sems("gathered", 4)
        w_loaded = sems("w_loaded", 2)
        xT_ready = sem("xT_ready")
        xh_ready = sem("xh_ready")
        xl_ready = sem("xl_ready")
        h_ready = sems("h_ready", HC)
        hf_ready = sems("hf_ready", HC)
        hh_ready = sems("hh_ready", HC)
        hl_ready = sems("hl_ready", HC)
        up_done = sem("up_done")
        yT_ready = sem("yT_ready")
        ytr_ready = sem("ytr_ready")
        y_ready = sem("y_ready")
        y_stored = sems("y_stored", 2)
        yg_in = sems("yg_in", 4)
        yg_used = sems("yg_used", 2)
        out_stored = sems("out_stored", 2)

        def layer_norm_scalars(ch, dve, st, mean_ap, out_ap, nmr_ap, scratch):
            v, half, y, a = scratch
            ch.add(dve.tensor_tensor(a, st[:, :, 1], st[:, :, 4], ALU.subtract))
            ch.add(dve.tensor_tensor(y, st[:, :, 2], st[:, :, 5], ALU.add))
            ch.then(dve.tensor_tensor(half, st[:, :, 1], st[:, :, 4], ALU.add))
            ch.add(dve.tensor_tensor(a, a, a, ALU.mult))
            ch.then(dve.tensor_scalar(mean_ap, half, 0.5, None, ALU.mult))
            ch.then(dve.scalar_tensor_tensor(a, a, C / 4, y, ALU.mult, ALU.add))
            ch.then(dve.tensor_scalar(a, a, 1.0 / C, None, ALU.mult))
            var = a
            ch.add(dve.tensor_scalar(v, var, EPS, None, ALU.add))
            ch.then(dve.tensor_scalar(half, var, -0.5, -0.5 * EPS, ALU.mult, ALU.add))
            ch.then(dve.tensor_scalar(y.bitcast(I32), v.bitcast(I32), -0.5, RSQRT_SEED, ALU.mult, ALU.add))
            for turn in range(3):
                ch.then(dve.tensor_tensor(a, y, y, ALU.mult))
                ch.then(dve.tensor_tensor(a, a, half, ALU.mult))
                ch.then(dve.scalar_tensor_tensor(out_ap if turn == 2 else y, a, 1.5, y, ALU.add, ALU.mult))
            ch.then(dve.scalar_tensor_tensor(nmr_ap, mean_ap, -1.0, out_ap, ALU.mult, ALU.mult))

        NBIAS = E * HC + E + 1

        def turn_bank(g):
            return bank[0] if g % 2 == 0 else bank[1]

        def logit_bank(part):
            return bank[(2, 6, 7, 3)[part]]

        def bias_pairs(dve, ch):
            dve.wait_ge(small_in[1], 16 * 9)
            ch.then(dve.tensor_copy(bhi[:], brow[:]))
            ch.add(dve.tensor_tensor(blo[:], brow[:], bhi[:].bitcast(F32), ALU.subtract))
            ch.then(dve.tensor_scalar(bsum[:], bhi[:].bitcast(F32), part01[:, 0:1], None, ALU.mult))
            ch.then(dve.scalar_tensor_tensor(bpair[:], blo[:].bitcast(F32), part01[:, 1:2], bsum[:], ALU.mult, ALU.add))

        class Route:

            def __init__(self, f, stage):
                self.f = f
                new = lambda name, shape, dt=F32: scoped(stage, f"{name}_{f}", shape, dt)
                self.L = new("logits", [P, NT, E])
                self.w = new("ranked", [P, NT, E])
                self.m = new("first", [P, NT])
                self.m2 = new("second", [P, NT])
                self.top = new("top", [P, NT])
                self.gap = new("gap", [P, NT])
                self.e2 = new("exp_gap_sb", [P, NT])
                self.choice = new("choice", [P, E, K, NT], BF16)
                self.pos = new("pos", [P, E, K * NT])
                self.cum = new("cum", [P, E, K * NT])
                self.base = new("base", [P, K * NT])
                self.at = new("at", [P, K * NT])
                self.at_i = new("at_i", [P, K * NT], I32)
                self.valid = new("valid", [P, K * NT])
                self.slotf = new("slotf", [P, K * NT])
                self.lof = new("lof", [P, K * NT])
                self.hif = new("hif", [P, K * NT])
                self.hi_oh = new("hi_oh", [P, K * NT, NCH])
                self.hi_tok = new("hi_tok", [P, K * NT, E * NCH], F32R)
                self.lo = new("lo", [P, 2, 16, P], F32R)
                self.away = new("away", [P, 2, 16 - LD, P])
                self.nlof = new("nlof", [P, K * NT])
                self.tok = new("tok", [E * NCH, P])
                self.xns = new("xns", [P, XB, GT, C])
                self.xnT = new("xnT", [P, 2, SEQ])

            def sync(self, sp):
                f = self.f
                for g in range(NG):
                    sp.wait_ge(norm_dve, NG * f + g + 1)
                    sp.wait_ge(norm_act, NG * f + g + 1)
                    sp.dma_start(rows(xn_dram, g * SEQ), self.xns[:, g % XB]).then_inc(xn_stored[g % XB], 16)
                for e in range(2):
                    if f == 0:
                        sp.wait_ge(exp_lo, e + 1)
                    sp.dma_start(wst[e][:].bitcast(F32), wres[:, e].bitcast(F32)).then_inc(w_loaded[e], 16)
                    if f == 0:
                        sp.wait_ge(WT_sb, 2)
                    sp.dma_start(bst[e][:], bcol[:, e * (HC + 1):(e + 1) * (HC + 1)]).then_inc(w_loaded[e], 16)
                for u in range(XB):
                    sp.wait_ge(xn_stored[u], 16 * NG // XB * (f + 1))
                for e in range(2):
                    sp.wait_ge(w_loaded[e], 32 * (E // 2 * f + 1))

            def buffer_free(self, eng, g):
                G = NG * self.f + g
                if g >= XB:
                    eng.wait_ge(xn_stored[g % XB], 16 * (G // XB))
                    eng.wait_ge(turned, G - XB + 1)

            def scalar_norm(self, act, between=lambda g: None):
                f = self.f

                def norm(g):
                    self.buffer_free(act, g)
                    t = GT * g + GT - 1
                    nc.scalar.activation(self.xns[:, g % XB, GT - 1], x_sb[:, t], ACT.Identity,
                                         bias=nmr[:, t:t + 1], scale=rstd[:, t:t + 1]).then_inc(norm_act, 1)

                def xnT_out(g):
                    act.wait_ge(turned, NG * f + g + 1)
                    if g >= 2:
                        act.wait_ge(logits_done, NG * f + g - 1)
                    nc.scalar.copy(self.xnT[:, g % 2], turn_bank(g)[:]).then_inc(xnT_ready, 1)

                act.wait_ge(rstd_done, f + 1)
                norm(0)
                norm(1)
                for g in range(NG):
                    if g + 2 < NG:
                        norm(g + 2)
                    xnT_out(g)
                    between(g)

            def scalar_gate(self, act):
                act.wait_ge(gap_done, self.f + 1)
                nc.scalar.activation(self.e2[:], self.gap[:], ACT.Exp).then_inc(exp_gap, 1)

            def tensor(self, pe):
                f = self.f

                def turn(g):
                    pe.wait_ge(norm_dve, NG * f + g + 1)
                    pe.wait_ge(norm_act, NG * f + g + 1)
                    if g >= 2:
                        pe.wait_ge(xnT_ready, NG * f + g - 1)
                    for t in range(GT):
                        last = nc.tensor.transpose(turn_bank(g)[:, t * P:(t + 1) * P], self.xns[:, g % XB, t], ident[:])
                    last.then_inc(turned, 1)

                def logits(g):
                    pe.wait_ge(xnT_ready, NG * f + g + 1)
                    for t in range(GT * g, GT * g + GT):
                        last = nc.tensor.matmul(logit_bank(g // 2)[:, t * E:(t + 1) * E], self.xnT[:, g % 2, (t % GT) * P:(t % GT + 1) * P],
                                                wg_sb[:], start=True, stop=True)
                    last.then_inc(logits_done, 1)

                turn(0)
                for g in range(NG):
                    if g + 1 < NG:
                        turn(g + 1)
                    logits(g)
                pe.wait_ge(gap_done, f + 1)
                flat = self.choice[:].rearrange("p e k t -> p (e k t)")
                nc.tensor.matmul(bank[3][:], tri[:], flat, start=True, stop=True)
                nc.tensor.matmul(bank[4][:], ones_bf[:], flat, start=True, stop=True).then_inc(counts_done, 1)
                for q in range(4):
                    Q = 4 * f + q
                    pe.wait_ge(hi_ready[min(q, 1)], f + 1 if q == 0 else 3 * f + q)
                    for j in range(16):
                        if j < LD and j % 4 == 0:
                            pe.wait_ge(lo_ready, LD // 4 * Q + j // 4 + 1)
                        elif j == LD:
                            pe.wait_ge(lo_act, Q + 1)
                        last = nc.tensor.matmul(bank[5][0:E * NCH, 0:P], self.hi_tok[:, 16 * q + j], self.lo[:, q % 2, j],
                                                start=(q == 0 and j == 0), stop=(q == 3 and j == 15))
                    last.then_inc(lo_used, 1)
                pe.wait_ge(tokens_copied, f + 1)
                nc.tensor.transpose(bank[0][:, 0:E * NCH], self.tok[:], ident[0:E * NCH, 0:E * NCH]).then_inc(inverse_done, 1)

            def expert_columns(self, eng, q):
                js = slice(16 * q, 16 * q + 16)
                ch2 = self.choice[:].rearrange("p e k t -> p (k t) e")
                eng.tensor_tensor(self.hi_tok[:, js].rearrange("p j (e h) -> p j e h", e=E),
                                  ch2[:, js].unsqueeze(3).to_broadcast([P, 16, E, NCH]),
                                  self.hi_oh[:, js].unsqueeze(2).to_broadcast([P, 16, E, NCH]), ALU.mult).then_inc(hi_ready[min(q, 1)], 1)

            def gpsimd_columns(self, gp):
                gp.wait_ge(slots_known, self.f + 1)
                for q in range(1, 4):
                    self.expert_columns(gp, q)

            def scalar_rows(self, act, ch):
                f = self.f
                act.wait_ge(slots_known, f + 1)
                for q in range(4):
                    Q = 4 * f + q
                    for j in range(16 - LD):
                        at = 16 * q + LD + j
                        ch.add(nc.scalar.activation(self.away[:, q % 2, j], iota_lo[:], ACT.Abs, bias=self.nlof[:, at:at + 1]))
                    ch.wait()
                    if Q >= 2:
                        act.wait_ge(lo_used, Q - 1)
                    nc.scalar.activation(self.lo[:, q % 2, LD:], self.away[:, q % 2], ACT.Relu, bias=1.0, scale=-1.0).then_inc(lo_act, 1)

            def top2(self, dve, ch, ts):
                n = ts.stop - ts.start
                L, w, top = self.L[:, ts], self.w[:, ts], self.top[:, ts]
                bt = lambda a: a.unsqueeze(2).to_broadcast([P, n, E])
                oh = [self.choice[:, :, k, ts].rearrange("p e t -> p t e") for k in range(K)]
                ch.then(dve.tensor_copy(L, logit_bank(ts.start // (2 * GT))[:, ts.start * E:ts.stop * E].rearrange("p (t e) -> p t e", e=E)))
                for k in range(K):
                    mk = (self.m if k == 0 else self.m2)[:, ts]
                    ch.then(dve.tensor_reduce(mk, L, AX, ALU.max))
                    ch.then(dve.tensor_tensor(w, L, bt(mk), ALU.is_equal))
                    ch.then(dve.tensor_tensor(w, w, prefer[:].unsqueeze(1).to_broadcast([P, n, E]), ALU.mult))
                    ch.then(dve.tensor_reduce(top, w, AX, ALU.max))
                    ch.then(dve.tensor_tensor(oh[k], w, bt(top), ALU.is_equal))
                    if k == 0:
                        ch.then(dve.scalar_tensor_tensor(L, oh[0], FAR, L, ALU.mult, ALU.add))

            def vector(self, dve, ch):
                f = self.f
                layer_norm_scalars(ch, dve, stats, mean[:], rstd[:], nmr[:], [nw[:, q] for q in range(4)])
                dve.tensor_copy(nw[:, 4, 0:1], nmr[:, 0:1]).then_inc(rstd_done, 1)
                for g in range(NG):
                    self.buffer_free(dve, g)
                    for t in range(GT * g, GT * g + GT - 1):
                        last = dve.tensor_scalar(self.xns[:, g % XB, t % GT], x_sb[:, t], mean[:, t:t + 1], rstd[:, t:t + 1], ALU.subtract, ALU.mult)
                    last.then_inc(norm_dve, 1)
                if f == 0:
                    dve.wait_ge(consts, 1)
                    bias_pairs(dve, ch)
                for g in range(1, NG, 2):
                    dve.wait_ge(logits_done, NG * f + g + 1)
                    self.top2(dve, ch, slice(GT * (g - 1), GT * (g + 1)))
                m, m2, gap, e2, choice = self.m, self.m2, self.gap, self.e2, self.choice
                dve.tensor_tensor(gap[:], m2[:], m[:], ALU.subtract).then_inc(gap_done, 1)
                ek = lambda a: a.unsqueeze(2).to_broadcast([P, E, K * NT])
                ch2 = choice[:].rearrange("p e k t -> p e (k t)")
                by_tok = lambda a: a.rearrange("p e j -> p j e")
                ch.add(dve.memset(self.cum[:, 0, 0:1], 0.0))
                ch.then(dve.tensor_tensor(self.pos[:], ch2, ek(expert_base[:]), ALU.mult))
                ch.then(dve.tensor_reduce(self.base[:], by_tok(self.pos[:]), AX, ALU.add))
                dve.wait_ge(counts_done, f + 1)
                fl = lambda a: a.rearrange("p e j -> p (e j)")
                ch.then(dve.tensor_tensor_scan(fl(self.cum[:])[:, 1:], bank[4][:, 0:E * K * NT - 1], fl(carry[:])[:, 1:], 0.0, ALU.add, ALU.mult))
                ch.then(dve.scalar_tensor_tensor(fl(self.cum[:]), bank[3][:], -1.0, fl(self.cum[:]), ALU.add, ALU.add))
                ch.then(dve.tensor_tensor(self.pos[:], self.cum[:], ch2, ALU.mult))
                ch.then(dve.tensor_reduce(self.at[:], by_tok(self.pos[:]), AX, ALU.add))
                ch.add(dve.tensor_copy(self.at_i[:], self.at[:]))
                ch.then(dve.tensor_scalar(self.valid[:], self.at[:], float(CAP), None, ALU.is_lt))
                ch.add(dve.tensor_scalar(self.at_i[:], self.at_i[:], P - 1, None, ALU.bitwise_and))
                ch.then(dve.tensor_tensor(self.slotf[:], self.at[:], self.valid[:], ALU.mult))
                ch.add(dve.tensor_copy(self.lof[:], self.at_i[:]))
                ch.then(dve.tensor_tensor(slot[:].rearrange("p k t -> p (k t)"), self.slotf[:], self.base[:], ALU.add))
                ch.then(dve.tensor_tensor(self.hif[:], self.at[:], self.lof[:], ALU.subtract))
                ch.then(dve.tensor_tensor(self.hi_oh[:], self.hif[:].unsqueeze(2).to_broadcast([P, K * NT, NCH]),
                                          iota_hi[:].unsqueeze(1).to_broadcast([P, K * NT, NCH]), ALU.is_equal))
                for k in range(K):
                    ch.add(dve.tensor_tensor(self.hi_oh[:, k * NT:(k + 1) * NT], self.hi_oh[:, k * NT:(k + 1) * NT],
                                             token_id[:].unsqueeze(2).to_broadcast([P, NT, NCH]), ALU.mult))
                ch.wait()
                dve.tensor_scalar(self.nlof[:], self.lof[:], -1.0, None, ALU.mult).then_inc(slots_known, 1)
                self.expert_columns(dve, 0)
                for q in range(4):
                    Q = 4 * f + q
                    if Q >= 2:
                        dve.wait_ge(lo_used, Q - 1)
                    for j in range(LD):
                        last = dve.tensor_scalar(self.lo[:, q % 2, j], iota_lo[:], self.lof[:, 16 * q + j:16 * q + j + 1], None, ALU.is_equal)
                        if j % 4 == 3:
                            last.then_inc(lo_ready, 1)
                dve.wait_ge(exp_gap, f + 1)
                gf = lambda k: gate[:, k]
                ch.then(dve.tensor_scalar(self.top[:], e2[:], 1.0, None, ALU.add))
                ch.then(dve.reciprocal(gap[:], self.top[:]))
                vk = lambda k: self.valid[:, k * NT:(k + 1) * NT]
                ch.add(dve.scalar_tensor_tensor(gf(0), gap[:], 0.5, vk(0), ALU.mult, ALU.mult))
                ch.then(dve.tensor_tensor(e2[:], e2[:], gap[:], ALU.mult))
                ch.then(dve.scalar_tensor_tensor(gf(1), e2[:], 0.5, vk(1), ALU.mult, ALU.mult))
                dve.wait_ge(lo_used, 4 * (f + 1))
                dve.tensor_copy(self.tok[:], bank[5][0:E * NCH, 0:P]).then_inc(tokens_copied, 1)
                dve.wait_ge(inverse_done, f + 1)
                ch.then(dve.tensor_copy(gidx[:], bank[0][:, 0:E * NCH]))

        class Experts:

            def __init__(self, f, stage):
                self.f, self.b = f, NSB * f
                new = lambda name, shape, dt=F32: scoped(stage, f"{name}_{f}", shape, dt)
                self.xg = new("xg", [P, 4, GT, C])
                self.xh = new("xh", [P, 2, 512], F32R)
                self.xl = new("xl", [P, 2, 512], F32R)
                self.hf = new("hf", [P, HC, 512])
                self.hh = new("hh", [P, 2, HC, 512], F32R)
                self.hl = new("hl", [P, 2, HC, 512], F32R)
                self.yT = new("yT", [P, 512])
                self.y_sb = new("y_sb", [P, 2, GT, C])

            def schedule(self, eng, step):
                step(0, 0)
                step(0, 1)
                if self.f == 0:
                    for r in range(2, 6):
                        step(0, r)
                with eng.Fori(1 if self.f == 0 else 0, 3) as i:
                    for r in range(2, 6):
                        step(i, r)
                for r in range(2, 6):
                    step(3, r)

            @staticmethod
            def has(i, r, d):
                if isinstance(i, int):
                    return 0 <= 4 * i + r - d < NSB
                return True

            def sync(self, sp):
                def step(i, r):
                    s = 4 * i + r
                    if self.has(i, r, 2):
                        sp.wait_ge(y_ready, self.b + s - 1)
                        sp.dma_start(rows(y_dram, (s - 2) * 512), self.y_sb[:, r % 2]).then_inc(y_stored[r % 2], 16)
                    if r % 2 == 0 and not (isinstance(i, int) and (s < 2 or s + 2 >= NSB)):
                        slot_ = (r // 2 + 1) % 2
                        sp.wait_ge(hl_free, self.b + s)
                        sp.dma_start(wst[slot_][:].bitcast(F32), wres[:, bass.ds(2 * i + r // 2 + 1, 1)].rearrange("p a w n -> p (a w) n").bitcast(F32)).then_inc(w_loaded[slot_], 16)
                        sp.wait_ge(yT_ready, self.b + s)
                        sp.dma_start(bst[slot_][:], bcol[:, bass.ds((2 * i + r // 2 + 1) * (HC + 1), HC + 1)]).then_inc(w_loaded[slot_], 16)
                self.schedule(sp, step)
                for u in range(2):
                    sp.wait_ge(y_stored[u], 16 * NSB // 2 * (self.f + 1))

            def gpsimd(self, gp):
                for s in range(NSB):
                    S = self.b + s
                    if S >= 4:
                        gp.wait_ge(xT_ready, S - 3)
                    for t in range(GT):
                        j = GT * s + t
                        gp.indirect_dma_start(out=self.xg[:, s % 4, t], out_offset=None, in_=xn_dram,
                                              in_offset=bass.IndirectOffsetOnAxis(ap=gidx[:, j:j + 1], axis=0)).then_inc(gathered[s % 4], 16)

            def tensor(self, pe):
                f, b = self.f, self.b

                def turn(i, r):
                    pe.wait_ge(gathered[r % 4], 64 * (4 * f + i + r // 4 + 1))
                    pe.wait_ge(xl_ready, b + 4 * i + r)
                    for t in range(GT):
                        last = nc.tensor.transpose(bank[0][:, t * P:(t + 1) * P], self.xg[:, r % 4, t], ident[:])
                    last.then_inc(xT_ready, 1)

                def up(i, r, c):
                    w = wst[(r // 2) % 2]
                    s = 4 * i + r
                    if c == 0:
                        pe.wait_ge(xl_ready, b + s + 1)
                        pe.wait_ge(w_loaded[(r // 2) % 2], 32 * (4 * f + i + r // 4 + 1))
                    pe.wait_ge(hf_ready[c], b + s)
                    at = slice(c * P, (c + 1) * P)
                    nc.tensor.matmul(bank[1 + c][:], w[:, 0, at], self.xh[:, r % 2], start=True, stop=False)
                    nc.tensor.matmul(bank[1 + c][:], w[:, 0, at], self.xl[:, r % 2], start=False, stop=False)
                    nc.tensor.matmul(bank[1 + c][:], w[:, 2, at], self.xh[:, r % 2], start=False, stop=True).then_inc(h_ready[c], 1)

                def down(i, r, c):
                    w = wst[(r // 2) % 2]
                    s = 4 * i + r
                    pe.wait_ge(hl_ready[c], b + s + 1)
                    sums = bank[5 + 2 * (r % 2)]
                    if c == 0 and not (isinstance(i, int) and b + s < 2):
                        pe.wait_ge(yT_ready, b + s - 1)
                    at = slice(c * P, (c + 1) * P)
                    nc.tensor.matmul(sums[:], w[:, 1, at], self.hh[:, r % 2, c], start=(c == 0), stop=False)
                    nc.tensor.matmul(sums[:], w[:, 1, at], self.hl[:, r % 2, c], start=False, stop=False)
                    last = nc.tensor.matmul(sums[:], w[:, 3, at], self.hh[:, r % 2, c], start=False, stop=(c == HC - 1))
                    if c == HC - 1:
                        last.then_inc(hl_free, 1)

                def back(i, r):
                    s = 4 * i + r
                    pe.wait_ge(yT_ready, b + s + 1)
                    pe.wait_ge(y_ready, b + s)
                    for t in range(GT):
                        last = nc.tensor.transpose(bank[6][:, t * P:(t + 1) * P], self.yT[:, t * P:(t + 1) * P], ident[:])
                    last.then_inc(ytr_ready, 1)

                def step(i, r):
                    for c in range(HC):
                        if self.has(i, r, 0):
                            up(i, r, c)
                        if c == 1 and self.has(i, r, 2):
                            back(i, r - 2)
                        if self.has(i, r, 1):
                            down(i, r - 1, c)
                        if c == 0 and self.has(i, r, -1):
                            turn(i, r + 1)
                turn(0, 0)
                self.schedule(pe, step)

            def scalar(self, act):
                f, b = self.f, self.b

                def high(i, r):
                    act.wait_ge(xT_ready, b + 4 * i + r + 1)
                    nc.scalar.copy(self.xh[:, r % 2], bank[0][:]).then_inc(xh_ready, 1)

                def step(i, r):
                    s = 4 * i + r
                    if self.has(i, r, 2):
                        act.wait_ge(hl_free, b + s - 1)
                        act.wait_ge(ytr_ready, b + s - 2)
                        nc.scalar.activation(self.yT[:], bank[5 + 2 * (r % 2)][:], ACT.Identity,
                                             bias=bst[(r // 2 + 1) % 2][:, HC:HC + 1]).then_inc(yT_ready, 1)
                    for c in range(HC):
                        if self.has(i, r, 0):
                            act.wait_ge(h_ready[c], b + s + 1)
                            act.wait_ge(hl_ready[c], b + s)
                            bias = bst[(r // 2) % 2][:, c:c + 1]
                            one = nc.scalar.activation(self.hf[:, c], bank[1 + c][:], ACT.Relu, bias=bias)
                            if c == HC - 1:
                                one = nc.scalar.activation(self.hh[:, r % 2, c], bank[1 + c][:], ACT.Relu, bias=bias)
                            one.then_inc(hf_ready[c], 1)
                        if c == 0 and self.has(i, r, -1):
                            high(i, r + 1)
                high(0, 0)
                self.schedule(act, step)

            def vector(self, dve):
                f, b = self.f, self.b

                def low(i, r):
                    dve.wait_ge(xh_ready, b + 4 * i + r + 1)
                    dve.tensor_tensor(self.xl[:, r % 2], bank[0][:], self.xh[:, r % 2].bitcast(F32), ALU.subtract).then_inc(xl_ready, 1)

                def step(i, r):
                    s = 4 * i + r
                    here = self.has(i, r, 0)

                    def h_high(c):
                        dve.wait_ge(hf_ready[c], b + s + 1)
                        dve.tensor_copy(self.hh[:, r % 2, c], self.hf[:, c]).then_inc(hh_ready[c], 1)

                    def h_low(c):
                        if c < HC - 1:
                            dve.wait_ge(hh_ready[c], b + s + 1)
                        else:
                            dve.wait_ge(hf_ready[c], b + s + 1)
                        dve.tensor_tensor(self.hl[:, r % 2, c], self.hf[:, c], self.hh[:, r % 2, c].bitcast(F32), ALU.subtract).then_inc(hl_ready[c], 1)
                    if here:
                        h_high(0)
                    if self.has(i, r, 2):
                        u = r % 2
                        dve.wait_ge(ytr_ready, b + s - 1)
                        dve.wait_ge(y_stored[u], 16 * (8 * f + 2 * i + (r - 2) // 2))
                        dve.tensor_copy(self.y_sb[:, u].rearrange("p t c -> p (t c)"), bank[6][:]).then_inc(y_ready, 1)
                    if here:
                        h_low(0)
                    if self.has(i, r, -1):
                        low(i, r + 1)
                    if here:
                        h_high(1)
                        h_high(2) if False else None
                        h_low(1)
                        h_high(2)
                        h_low(2)
                        h_low(3)
                low(0, 0)
                self.schedule(dve, step)

        hl_free = sem("hl_free")

        ones_col = sem("ones_col")
        an_stats = sem("an_stats")
        an_scale = sem("an_scale")
        an_ready = sem("an_ready")
        an_turned = sem("an_turned")
        anT_ready = sem("anT_ready")
        q_ready = sem("q_ready")
        q_split = sem("q_split")
        q_parts = sem("q_parts")
        qT_ready = sem("qT_ready")
        kv_ready = sem("kv_ready")
        k_split = sem("k_split")
        k_parts = sem("k_parts")
        v_copied = sem("v_copied")
        k_rows = sem("k_rows")
        keysum_ready = sem("keysum_ready")
        kv_masked = sem("kv_masked")
        num_ready = sem("num_ready")
        den_step = sem("den_step")
        att_ready = sem("att_ready")
        att_turned = sem("att_turned")
        attT_ready = sem("attT_ready")
        o_ready = sem("o_ready")
        x_summed = sem("x_summed")
        new_stats = sem("new_stats")

        class Gather:

            def __init__(self, stage, f):
                self.f = f
                self.yg = scoped(stage, f"yg_{f}", [P, 2, K, GT, C])

            def gpsimd(self, gp):
                f = self.f
                for n in range(NG):
                    u = n % 2
                    for k in range(K):
                        if f * NG + n >= 2:
                            gp.wait_ge(yg_used[k], NG * f + n - 1)
                        for t in range(GT):
                            gp.indirect_dma_start(out=self.yg[:, u, k, t], out_offset=None, in_=y_dram,
                                                  in_offset=bass.IndirectOffsetOnAxis(ap=slot[:, k, GT * n + t:GT * n + t + 1], axis=0)).then_inc(yg_in[2 * u + k], 16)

        class Attention:

            STEPS = NG + 3

            def __init__(self, stage, gather):
                new = lambda name, shape: scoped(stage, name, shape)
                self.yg = gather.yg
                self.an = new("an", [P, 2, GT, C])
                self.anT = new("anT", [P, 2, SEQ])
                self.qe = new("qe", [P, 2, SEQ])
                self.qr = new("qr", [P, 2, SEQ])
                self.ke = new("ke", [P, 2, SEQ])
                self.kr = new("kr", [P, 2, SEQ])
                self.qT = new("qT", [P, 2, SEQ])
                self.kk = new("kk", [P, 2, GT, C])
                self.vv = new("vv", [P, 2, GT, C + 1])
                self.kv = new("kv", [P, 2, C + HEADS])
                self.den = new("den", [P, 2, GT, HEADS])
                self.att = new("att", [P, 2, GT, C])
                self.attT = new("attT", [P, 2, SEQ])
                self.sta = new("sta", [P, 2, GT, 6])
                self.agg = new("agg", [P, 2, GT, 2])
                self.nwa = new("nwa", [P, 2, 3, GT])
                self.rsa = new("rsa", [P, 2, 2, GT])

            def tensor(self, pe):
                def turn_out(n):
                    pe.wait_ge(att_ready, n + 1)
                    if n >= 1:
                        pe.wait_ge(attT_ready, n)
                    for t in range(GT):
                        last = nc.tensor.transpose(bank[6][:, t * P:(t + 1) * P], self.att[:, n % 2, t], ident[:])
                    last.then_inc(att_turned, 1)

                def turn(n):
                    pe.wait_ge(an_ready, n + 1)
                    if n >= 1:
                        pe.wait_ge(anT_ready, n)
                    for t in range(GT):
                        last = nc.tensor.transpose(bank[0][:, t * P:(t + 1) * P], self.an[:, n % 2, t], ident[:])
                    last.then_inc(an_turned, 1)

                def project(n):
                    pe.wait_ge(attT_ready, n + 1)
                    if n >= 1:
                        pe.wait_ge(x_summed, n)
                    for t in range(GT):
                        at = slice(t * P, (t + 1) * P)
                        nc.tensor.matmul(bank[7][:, at], self.attT[:, n % 2, at], WT[:, 3], start=True, stop=False)
                        last = nc.tensor.matmul(bank[7][:, at], ones2[:], bpair[:, 2], start=False, stop=True)
                    last.then_inc(o_ready, 1)

                def keysum(n):
                    pe.wait_ge(k_rows, n + 1)
                    pe.wait_ge(v_copied, n + 1)
                    if n == 0:
                        pe.wait_ge(ones_col, 1)
                    else:
                        pe.wait_ge(att_ready, n)
                    for t in range(GT):
                        last = nc.tensor.matmul(bank[4][:, 0:C + 1], self.kk[:, n % 2, t], self.vv[:, n % 2, t], start=(t == 0), stop=(t == GT - 1))
                    last.then_inc(keysum_ready, 1)

                def q(n):
                    pe.wait_ge(anT_ready, n + 1)
                    if n >= 1:
                        pe.wait_ge(q_parts, n)
                    nc.tensor.matmul(bank[1][:], WT[:, 0], self.anT[:, n % 2], start=True, stop=True).then_inc(q_ready, 1)

                def query(n):
                    pe.wait_ge(kv_masked, 2 * n + 2)
                    pe.wait_ge(qT_ready, n + 1)
                    if n >= 1:
                        pe.wait_ge(att_ready, n)
                    for t in range(GT):
                        at = slice(t * P, (t + 1) * P)
                        nc.tensor.matmul(bank[5][:, at], self.qT[:, n % 2, at], self.kv[:, n % 2, 0:C], start=True, stop=True)
                        last = nc.tensor.matmul(bank[4][:, 256 + t * HEADS:256 + (t + 1) * HEADS], self.qT[:, n % 2, at],
                                                self.kv[:, n % 2, C:C + HEADS], start=True, stop=True)
                    last.then_inc(num_ready, 1)

                def kv(n):
                    if n >= 1:
                        pe.wait_ge(k_parts, n)
                        pe.wait_ge(v_copied, n)
                    for w in (0, 1):
                        for t in range(GT):
                            at = slice(t * P, (t + 1) * P)
                            nc.tensor.matmul(bank[2 + w][:, at], self.anT[:, n % 2, at], WT[:, 1 + w], start=True, stop=False)
                            last = nc.tensor.matmul(bank[2 + w][:, at], ones2[:], bpair[:, w], start=False, stop=True)
                        last.then_inc(kv_ready, 1)

                for s in range(self.STEPS):
                    middle, late = 2 <= s <= NG + 1, 3 <= s <= NG + 2
                    if 1 <= s <= NG:
                        turn(s - 1)
                    if late:
                        turn_out(s - 3)
                    if 1 <= s <= NG:
                        q(s - 1)
                    if middle:
                        keysum(s - 2)
                    if 1 <= s <= NG:
                        kv(s - 1)
                    if middle:
                        query(s - 2)
                    if late:
                        project(s - 3)

            def scalar(self, act):
                def attT_out(n):
                    act.wait_ge(att_turned, n + 1)
                    if n >= 2:
                        act.wait_ge(o_ready, n - 1)
                    nc.scalar.copy(self.attT[:, n % 2], bank[6][:]).then_inc(attT_ready, 1)

                def norm(n):
                    act.wait_ge(an_scale, n + 1)
                    if n >= 2:
                        act.wait_ge(an_turned, n - 1)
                    for t in range(GT):
                        last = nc.scalar.activation(self.an[:, n % 2, t], x_sb[:, GT * n + t], ACT.Identity,
                                                    bias=self.rsa[:, n % 2, 1, t:t + 1], scale=self.rsa[:, n % 2, 0, t:t + 1])
                    last.then_inc(an_ready, 1)

                def anT_out(n):
                    act.wait_ge(an_turned, n + 1)
                    if n >= 2:
                        act.wait_ge(kv_ready, 2 * (n - 1))
                    nc.scalar.copy(self.anT[:, n % 2], bank[0][:]).then_inc(anT_ready, 1)

                def q_act(n):
                    u = n % 2
                    act.wait_ge(q_ready, n + 1)
                    if n >= 2:
                        act.wait_ge(qT_ready, n - 1)
                    nc.scalar.activation(self.qe[:, u], bank[1][:], ACT.Relu, bias=nbq[:], scale=-1.0).then_inc(q_split, 1)
                    nc.scalar.activation(self.qr[:, u], bank[1][:], ACT.Relu, bias=bcol[:, NBIAS - 1:NBIAS])
                    act.wait_ge(q_split, n + 1)
                    nc.scalar.activation(self.qe[:, u], self.qe[:, u], ACT.Exp, scale=-1.0).then_inc(q_parts, 1)

                def k_act(n):
                    u = n % 2
                    act.wait_ge(kv_ready, 2 * n + 1)
                    if n >= 2:
                        act.wait_ge(k_rows, n - 1)
                    nc.scalar.activation(self.ke[:, u], bank[2][:], ACT.Relu, scale=-1.0).then_inc(k_split, 1)
                    nc.scalar.activation(self.kr[:, u], bank[2][:], ACT.Relu)
                    act.wait_ge(k_split, n + 1)
                    nc.scalar.activation(self.ke[:, u], self.ke[:, u], ACT.Exp, scale=-1.0).then_inc(k_parts, 1)

                def v_out(n):
                    act.wait_ge(kv_ready, 2 * n + 2)
                    if n >= 2:
                        act.wait_ge(keysum_ready, n - 1)
                    nc.scalar.copy(self.vv[:, n % 2, :, 0:C], bank[3][:].rearrange("p (t c) -> p t c", c=C)).then_inc(v_copied, 1)

                for s in range(self.STEPS):
                    if 1 <= s <= NG:
                        norm(s - 1)
                        anT_out(s - 1)
                        q_act(s - 1)
                    if 3 <= s <= NG + 2:
                        attT_out(s - 3)
                    if 1 <= s <= NG:
                        k_act(s - 1)
                        v_out(s - 1)

            def vector(self, dve, ch):
                def add_rows(n, k, t):
                    if t == 0:
                        dve.wait_ge(yg_in[2 * (n % 2) + k], 64 * (n // 2 + 1))
                        if k == 1:
                            dve.wait_ge(yg_used[0], n + 1)
                    at = GT * n + t
                    one = dve.scalar_tensor_tensor(x_sb[:, at], self.yg[:, n % 2, k, t], gate[:, k, at:at + 1], x_sb[:, at], ALU.mult, ALU.add)
                    if t == GT - 1:
                        one.then_inc(yg_used[k], 1)

                def an_statistics(n):
                    dve.wait_ge(yg_used[1], n + 1)
                    if n >= 2:
                        dve.wait_ge(an_ready, n - 1)
                    for t in range(GT):
                        last = dve.bn_stats(self.sta[:, n % 2, t], x_sb[:, GT * n + t])
                    last.then_inc(an_stats, 1)

                def scale_steps(n):
                    u = n % 2
                    v, y, a = (self.nwa[:, u, q] for q in range(3))
                    dve.wait_ge(an_stats, n + 1)
                    for t in range(GT):
                        ch.add(dve.bn_aggr(self.agg[:, u, t], self.sta[:, u, t]))
                    done = ch.n
                    yield
                    ch.wait(done)
                    ch.add(dve.tensor_scalar(v, self.agg[:, u, :, 1], EPS, None, ALU.add))
                    done = ch.n
                    yield
                    ch.wait(done)
                    ch.add(dve.tensor_scalar(y.bitcast(I32), v.bitcast(I32), -0.5, NEG_EIGHTH_SEED, ALU.mult, ALU.add))
                    done = ch.n
                    yield
                    for square in (64.0, 16.0, 4.0):
                        ch.wait(done)
                        ch.add(dve.scalar_tensor_tensor(a, y, square, y, ALU.mult, ALU.mult))
                        done = ch.n
                        yield
                        ch.wait(done)
                        ch.add(dve.tensor_tensor(a, a, v, ALU.mult))
                        done = ch.n
                        yield
                        ch.wait(done)
                        to = self.rsa[:, u, 0] if square == 4.0 else y
                        ch.add(dve.scalar_tensor_tensor(to, a, -3.0, y, ALU.add, ALU.mult))
                        done = ch.n
                        yield
                    ch.wait(done)
                    dve.scalar_tensor_tensor(self.rsa[:, u, 1], self.agg[:, u, :, 0], -1.0, self.rsa[:, u, 0], ALU.mult, ALU.mult).then_inc(an_scale, 1)
                    yield

                def k_sum(n):
                    dve.wait_ge(k_parts, n + 1)
                    if n >= 2:
                        dve.wait_ge(keysum_ready, n - 1)
                    dve.tensor_tensor(self.kk[:, n % 2].rearrange("p t c -> p (t c)"), self.ke[:, n % 2], self.kr[:, n % 2], ALU.add).then_inc(k_rows, 1)

                def q_sum(n):
                    dve.wait_ge(q_parts, n + 1)
                    if n >= 2:
                        dve.wait_ge(num_ready, n - 1)
                    dve.tensor_tensor(self.qT[:, n % 2], self.qe[:, n % 2], self.qr[:, n % 2], ALU.add).then_inc(qT_ready, 1)

                def kv_mask(n):
                    u = n % 2
                    dve.wait_ge(keysum_ready, n + 1)
                    if n >= 2:
                        dve.wait_ge(num_ready, n - 1)
                    dve.tensor_tensor(self.kv[:, u, 0:C], bank[4][:, 0:C], block_mask[:], ALU.mult).then_inc(kv_masked, 1)
                    dve.tensor_tensor(self.kv[:, u, C:C + HEADS], head_mask[:], bank[4][:, C:C + 1].to_broadcast([P, HEADS]), ALU.mult).then_inc(kv_masked, 1)

                def den_max(n):
                    dve.wait_ge(num_ready, n + 1)
                    dve.tensor_scalar(self.den[:, n % 2], bank[4][:, 256:256 + GT * HEADS].rearrange("p (t h) -> p t h", h=HEADS), 1e-6, None, ALU.max).then_inc(den_step, 1)

                def den_inverse(n):
                    dve.wait_ge(den_step, 2 * n + 1)
                    dve.reciprocal(self.den[:, n % 2], self.den[:, n % 2]).then_inc(den_step, 1)

                def divide(n):
                    u = n % 2
                    dve.wait_ge(den_step, 2 * n + 2)
                    if n >= 2:
                        dve.wait_ge(att_turned, n - 1)
                    dve.tensor_tensor(self.att[:, u].rearrange("p t (h d) -> p (t h) d", d=HD), bank[5][:].rearrange("p (a d) -> p a d", d=HD),
                                      self.den[:, u].rearrange("p t h -> p (t h)").unsqueeze(2).to_broadcast([P, GT * HEADS, HD]), ALU.mult).then_inc(att_ready, 1)

                def residual(n):
                    dve.wait_ge(o_ready, n + 1)
                    xb = x_sb[:, GT * n:GT * n + GT]
                    dve.tensor_tensor(xb, bank[7][:].rearrange("p (t c) -> p t c", c=C), xb, ALU.add).then_inc(x_summed, 1)

                def statistics(n):
                    dve.wait_ge(x_summed, n + 1)
                    for t in range(GT * n, GT * n + GT):
                        last = dve.bn_stats(stats[:, t], x_sb[:, t])
                    last.then_inc(new_stats, 1)

                for k in range(K):
                    for t in range(GT):
                        add_rows(0, k, t)
                for s in range(self.STEPS):
                    front, middle = s < NG, 2 <= s <= NG + 1
                    if middle:
                        k_sum(s - 2)
                    if front:
                        an_statistics(s)
                    scale = scale_steps(s) if front else iter(())
                    next(scale, None)
                    if s == 0:
                        for _ in scale:
                            pass
                    for k in range(K):
                        for t in range(GT):
                            if s + 1 < NG:
                                add_rows(s + 1, k, t)
                            next(scale, None)
                        if k == 0 and middle:
                            kv_mask(s - 2)
                    for _ in scale:
                        pass
                    if 1 <= s <= NG:
                        q_sum(s - 1)
                    for n in {NG: (0, 1), NG + 1: (2, 3, 4), NG + 2: (5, 6)}.get(s, ()):
                        statistics(n)
                    if middle:
                        den_max(s - 2)
                        den_inverse(s - 2)
                        divide(s - 2)
                    if s >= 3:
                        residual(s - 3)
                statistics(NG - 1)
                dve.wait_ge(new_stats, NG)

        chain = [None]

        def dve_chain(dve):
            if chain[0] is None:
                chain[0] = Chain(dve, dve_step)
            chain[0].eng = dve
            return chain[0]

        act_steps = [None]

        def act_chain(act):
            if act_steps[0] is None:
                act_steps[0] = Chain(act, act_step)
            act_steps[0].eng = act
            return act_steps[0]

        with ExitStack() as stage, nc.Block() as block:
            route = Route(0, stage)
            wexp_raw = scoped(stage, "wexp_raw", [P, RB, 2, H])
            wraw = scoped(stage, "wraw", [P, 4, C])
            brows = scoped(stage, "brows", [NBIAS, P])

            def load_expert(eng, e):
                eng.dma_start(wexp_raw[:, e % RB, 0], w1[e]).then_inc(exp_raw_in[e], 16)
                eng.dma_start(wexp_raw[:, e % RB, 1].rearrange("p (c m) -> p c m", m=C), w2[e].rearrange("(c p) m -> p c m", p=P)).then_inc(exp_raw_in[e], 16)

            @block.sync
            def _(sp):
                for g in range(NG):
                    if g >= 4:
                        sp.wait_ge(x_arrived[g % 4], 16)
                    sp.dma_start(x_sb[:, g * GT:(g + 1) * GT, :], rows(xf, g * SEQ)).then_inc(x_arrived[g % 4], 16)
                for e in range(RB):
                    load_expert(sp, e)
                route.sync(sp)

            @block.gpsimd
            def _(gp):
                ch = Chain(gp, const_chain)
                ch.add(nc.gpsimd.memset(ident[:], 0.0))
                ch.add(nc.gpsimd.memset(tri[:], 1.0))
                ch.add(nc.gpsimd.memset(head_mask[:], 1.0))
                ch.add(nc.gpsimd.memset(ones_row[:], 1.0))
                ch.add(nc.gpsimd.memset(part01[:], 0.0))
                ch.add(nc.gpsimd.memset(ones_bf[:], 1.0))
                ch.then(nc.gpsimd.memset(carry[:], 1.0))
                fl = dict(allow_small_or_imprecise_dtypes=True)
                ch.add(nc.gpsimd.affine_select(out=ident[:], in_=ident[:], compare_op=ALU.not_equal, fill=1.0, base=0, pattern=[[-1, P]], channel_multiplier=1))
                ch.add(nc.gpsimd.affine_select(out=tri[:], in_=tri[:], compare_op=ALU.is_ge, fill=0.0, base=0, pattern=[[1, P]], channel_multiplier=-1))
                ch.add(nc.gpsimd.affine_select(out=part01[:], in_=part01[:], compare_op=ALU.not_equal, fill=1.0, base=0, pattern=[[-1, 2]], channel_multiplier=1))
                ch.add(nc.gpsimd.memset(carry[:, :, 0:1], 0.0))
                ch.then(nc.gpsimd.affine_select(out=head_mask[:], in_=head_mask[:], compare_op=ALU.is_ge, fill=0.0, base=0, pattern=[[-HD, HEADS]], channel_multiplier=1))
                ch.then(nc.gpsimd.affine_select(out=head_mask[:], in_=head_mask[:], compare_op=ALU.is_ge, fill=0.0, base=HD - 1, pattern=[[HD, HEADS]], channel_multiplier=-1))
                ch.add(nc.gpsimd.tensor_copy(block_mask[:].rearrange("p (h d) -> p h d", d=HD), head_mask[:].unsqueeze(2).to_broadcast([P, HEADS, HD])))
                ch.add(nc.gpsimd.iota(iota_lo[:], pattern=[[1, P]], base=0, channel_multiplier=0, **fl))
                ch.add(nc.gpsimd.iota(prefer[:], pattern=[[-1, E]], base=E, channel_multiplier=0, **fl))
                ch.add(nc.gpsimd.iota(iota_hi[:], pattern=[[P, NCH]], base=0, channel_multiplier=0, **fl))
                ch.add(nc.gpsimd.iota(expert_base[:], pattern=[[CAP, E]], base=0, channel_multiplier=0, **fl))
                ch.then(nc.gpsimd.iota(token_id[:], pattern=[[P, NT]], base=0, channel_multiplier=1, **fl))
                nc.gpsimd.tensor_copy(ones2[:], ones_row[:]).then_inc(consts, 1)
                for e in range(E):
                    gp.wait_ge(exp_hi, e + 1)
                    nc.gpsimd.tensor_tensor(wres[:, e, 2:4], wexp_raw[:, e % RB], wres[:, e, 0:2].bitcast(F32), ALU.subtract).then_inc(exp_lo, 1)
                    if e + RB < E:
                        gp.wait_ge(exp_lo, e + 1)
                        load_expert(gp, e + RB)
                route.gpsimd_columns(gp)

            @block.scalar
            def _(act):
                for j, W in enumerate((Wq, Wk, Wv, Wo)):
                    act.dma_start(wraw[:, j], W).then_inc(small_in[0], 16)
                act.dma_start(wg_sb[:], wg).then_inc(small_in[2], 16)
                act.dma_start(brows[0:E * HC], b1.rearrange("e (c p) -> (e c) p", p=P)).then_inc(small_in[1], 16)
                act.dma_start(brows[E * HC:E * HC + E], b2).then_inc(small_in[1], 16)
                act.dma_start(brows[NBIAS - 1:NBIAS], bq.rearrange("(a n) -> a n", a=1)).then_inc(small_in[1], 16)
                for j, bias in enumerate((bk, bv, bo)):
                    for row in range(2):
                        act.dma_start(brow[row:row + 1, j], bias.rearrange("(a n) -> a n", a=1)).then_inc(small_in[1], 16)
                act.wait_ge(WT_ps, 1)
                nc.scalar.copy(WT[:].rearrange("p w c -> p (w c)"), bank[6][:]).then_inc(WT_sb, 1)
                by_expert = bcol[:, 0:E * (HC + 1)].rearrange("p (e c) -> p e c", c=HC + 1)
                nc.scalar.copy(by_expert[:, :, 0:HC], bank[7][:, 0:E * HC].rearrange("p (e c) -> p e c", c=HC))
                nc.scalar.copy(by_expert[:, :, HC], bank[7][:, E * HC:E * HC + E])
                nc.scalar.copy(bcol[:, NBIAS - 1:NBIAS], bank[7][:, NBIAS - 1:NBIAS])
                nc.scalar.mul(nbq[:], bank[7][:, NBIAS - 1:NBIAS], -1.0).then_inc(WT_sb, 1)

                def high_part(e):
                    act.wait_ge(exp_raw_in[e], 32)
                    nc.scalar.copy(wres[:, e, 0:2], wexp_raw[:, e % RB]).then_inc(exp_hi, 1)

                route.scalar_norm(act, lambda g: high_part(g - 1) if 1 <= g <= RB else None)
                for e in range(RB, E):
                    high_part(e)
                route.scalar_gate(act)
                route.scalar_rows(act, act_chain(act))

            @block.tensor
            def _(pe):
                pe.wait_ge(consts, 1)
                pe.wait_ge(small_in[0], 64)
                for j in range(4):
                    nc.tensor.transpose(bank[6][:, j * P:(j + 1) * P], wraw[:, j], ident[:])
                pe.wait_ge(small_in[1], 16 * 9)
                nc.tensor.transpose(bank[7][:, 0:NBIAS], brows[:], ident[0:NBIAS, 0:NBIAS]).then_inc(WT_ps, 1)
                pe.wait_ge(small_in[2], 16)
                route.tensor(pe)

            @block.vector
            def _(dve):
                ch = dve_chain(dve)
                for g in range(NG):
                    dve.wait_ge(x_arrived[g % 4], 16 * (g // 4 + 1))
                    for t in range(GT * g, GT * g + GT):
                        ch.add(dve.bn_stats(stats[:, t], x_sb[:, t]))
                ch.wait()
                route.vector(dve, ch)

        def experts_block(f):
            with ExitStack() as stage, nc.Block() as block:
                experts = Experts(f, stage)

                @block.sync
                def _(sp):
                    experts.sync(sp)

                @block.gpsimd
                def _(gp):
                    experts.gpsimd(gp)

                @block.tensor
                def _(pe):
                    experts.tensor(pe)

                @block.scalar
                def _(act):
                    experts.scalar(act)

                @block.vector
                def _(dve):
                    experts.vector(dve)

        experts_block(0)

        with ExitStack() as stage, nc.Block() as block:
            gather = Gather(stage, 0)
            attention = Attention(stage, gather)

            @block.gpsimd
            def _(gp):
                nc.gpsimd.memset(attention.vv[:, :, :, C:C + 1], 1.0).then_inc(ones_col, 1)
                gather.gpsimd(gp)

            @block.tensor
            def _(pe):
                attention.tensor(pe)

            @block.scalar
            def _(act):
                attention.scalar(act)

            @block.vector
            def _(dve):
                attention.vector(dve, dve_chain(dve))

        with ExitStack() as stage, nc.Block() as block:
            route = Route(1, stage)

            @block.sync
            def _(sp):
                route.sync(sp)

            @block.scalar
            def _(act):
                route.scalar_norm(act)
                route.scalar_gate(act)
                route.scalar_rows(act, act_chain(act))

            @block.gpsimd
            def _(gp):
                route.gpsimd_columns(gp)

            @block.tensor
            def _(pe):
                route.tensor(pe)

            @block.vector
            def _(dve):
                route.vector(dve, dve_chain(dve))

        experts_block(1)

        with ExitStack() as stage, nc.Block() as block:
            gather = Gather(stage, 1)
            last = scoped(stage, "last", [P, 2, GT, C])

            @block.gpsimd
            def _(gp):
                gather.gpsimd(gp)

            @block.vector
            def _(dve):
                for n in range(NG):
                    u = n % 2
                    for k in range(K):
                        dve.wait_ge(yg_in[2 * u + k], 64 * ((NG + n) // 2 + 1))
                        if k == 1:
                            dve.wait_ge(yg_used[0], NG + n + 1)
                        elif n >= 2:
                            dve.wait_ge(out_stored[u], 16 * (n // 2))
                        for t in range(GT):
                            at = GT * n + t
                            one = dve.scalar_tensor_tensor(last[:, u, t], gather.yg[:, u, k, t], gate[:, k, at:at + 1],
                                                           x_sb[:, at] if k == 0 else last[:, u, t], ALU.mult, ALU.add)
                        one.then_inc(yg_used[k], 1)

            @block.sync
            def _(sp):
                for n in range(NG):
                    sp.wait_ge(yg_used[1], NG + n + 1)
                    sp.dma_start(rows(of, n * SEQ), last[:, n % 2]).then_inc(out_stored[n % 2], 16)
                for u in range(2):
                    sp.wait_ge(out_stored[u], 16 * NG // 2)


_INS = ["L0_attn_x", "L0_attn_Wq", "L0_attn_bq", "L0_attn_Wk", "L0_attn_bk", "L0_attn_Wv", "L0_attn_bv", "L0_attn_Wo",
        "L0_attn_bo", "L0_ffn_wg", "L0_ffn_w1", "L0_ffn_b1", "L0_ffn_w2", "L0_ffn_b2"]
_OUTS = [((8, 512, 128), "float32")]


def kernel(**inputs):
    import numpy as _np
    import concourse.bacc as _bacc
    from concourse import mybir as _mybir
    from concourse.bass_utils import run_bass_kernel_spmd as _run

    nc = _bacc.Bacc("TRN2", target_bir_lowering=False, num_devices=1)
    arrays, args = {}, []
    for name in _INS:
        a = _np.ascontiguousarray(inputs[name])
        arrays[f"in_{name}"] = a
        args.append(nc.dram_tensor(f"in_{name}", a.shape, _mybir.dt.from_np(a.dtype), kind="ExternalInput").ap())
    for i, (shape, dtype) in enumerate(_OUTS):
        args.append(nc.dram_tensor(f"out_{i}", shape, _mybir.dt.from_np(_np.dtype(dtype)), kind="ExternalOutput").ap())
    macaron(nc, *args)
    r = _run(nc, [arrays], core_ids=[0])
    return r.results[0]["out_0"]
```

```python
import concourse.bass as bass
from concourse import mybir
from contextlib import ExitStack

F32 = mybir.dt.float32
F32R = mybir.dt.float32r
BF16 = mybir.dt.bfloat16
I32 = mybir.dt.int32
ALU = mybir.AluOpType
ACT = mybir.ActivationFunctionType
AX = mybir.AxisListType.X

P = 128
NB, SEQ, C = 8, 512, 128
N = NB * SEQ
NT = N // P
GT = SEQ // P
NG = NT // GT
E, K, H = 8, 2, 512
HC = H // P
LD = 13
EARLY = (NG // 2, NG // 2)
XB = 4
RB = 4
CAP = K * N // E
NCH = CAP // P
NSB = E * CAP // 512
HEADS, HD = 16, 8
EPS = 1e-5
FAR = -3e38
RSQRT_SEED = 1597463007.0
NEG_EIGHTH_SEED = RSQRT_SEED - 3 * 2.0 ** 23 - 2.0 ** 31


class Chain:

    def __init__(self, eng, sem):
        self.eng, self.sem, self.n = eng, sem, 0

    def add(self, ins):
        ins.then_inc(self.sem, 1)
        self.n += 1

    def wait(self, n=None):
        self.eng.wait_ge(self.sem, self.n if n is None else n)

    def then(self, ins):
        self.add(ins)
        self.wait()


def finish(steps):
    for _ in steps:
        pass


def macaron(nc, x_in, Wq, bq, Wk, bk, Wv, bv, Wo, bo, wg, w1, b1, w2, b2, out):
    ctx = ExitStack()
    with ctx:
        def sb(name, shape, dt=F32):
            return ctx.enter_context(nc.sbuf_tensor(name, shape, dt))

        def scoped(stage, name, shape, dt=F32):
            return stage.enter_context(nc.sbuf_tensor(name, shape, dt))

        def sem(name):
            return ctx.enter_context(nc.semaphore(name))

        def sems(name, n):
            return [sem(f"{name}{i}") for i in range(n)]

        xf = x_in.rearrange("b s c -> (b s) c")
        of = out.rearrange("b s c -> (b s) c")
        xn_dram = nc.dram_tensor("xn_dram", (N, C), F32, kind="Internal").ap()
        y_dram = nc.dram_tensor("y_dram", (E * CAP, C), F32, kind="Internal").ap()

        def rows(dram, at, tiles=GT):
            return dram[bass.ds(at, tiles * P), :].rearrange("(t p) c -> p t c", p=P)

        ident = sb("ident", [P, P])
        tri = sb("tri", [P, P], BF16)
        ones_bf = sb("ones_bf", [P, P], BF16)
        iota_lo = sb("iota_lo", [P, P])
        prefer = sb("prefer", [P, E])
        iota_hi = sb("iota_hi", [P, NCH])
        expert_base = sb("expert_base", [P, E])
        token_id = sb("token_id", [P, NT])
        carry = sb("carry", [P, E, K * NT])
        head_mask = sb("head_mask", [P, HEADS])
        block_mask = sb("block_mask", [P, P])
        ones_row = sb("ones_row", [2, P])
        ones2 = sb("ones2", [2, P], F32R)
        part01 = sb("part01", [2, 2])
        wg_sb = sb("wg_sb", [P, E])
        WT = sb("WT", [P, 4, C])
        bcol = sb("bcol", [P, E * (HC + 1) + 1])
        nbq = sb("nbq", [P, 1])
        brow = sb("brow", [2, 3, C])
        bhi = sb("bhi", [2, 3, C], F32R)
        blo = sb("blo", [2, 3, C], F32R)
        bsum = sb("bsum", [2, 3, C])
        bpair = sb("bpair", [2, 3, C], F32R)
        wres = sb("wres", [P, E, 4, H], F32R)
        bst = [sb(f"bst{i}", [P, HC + 1]) for i in range(2)]
        wst = [sb(f"wst{i}", [P, 4, H], F32R) for i in range(2)]
        x_sb = sb("x_sb", [P, NT, C])
        stats = sb("stats", [P, NT, 6])
        mean = sb("mean", [P, NT])
        nw = sb("nw", [P, 4, NT])
        rstd = sb("rstd", [P, NT])
        nmr = sb("nmr", [P, NT])
        gate = sb("gate", [P, K, NT])
        slot = sb("slot", [P, K, NT], I32)
        gidx = sb("gidx", [P, E * NCH], I32)

        bank = [ctx.enter_context(nc.psum_tensor(f"bank{i}", [P, 512], F32)) for i in range(8)]

        consts = sem("consts")
        const_chain = sem("const_chain")
        small_in = sems("small_in", 3)
        x_arrived = sems("x_arrived", 4)
        exp_raw_in = sems("exp_raw_in", E)
        exp_hi = sem("exp_hi")
        exp_lo = sem("exp_lo")
        WT_ps = sem("WT_ps")
        WT_sb = sem("WT_sb")
        dve_step = sem("dve_step")
        act_step = sem("act_step")
        rstd_done = sem("rstd_done")
        norm_dve = sem("norm_dve")
        norm_act = sem("norm_act")
        turned = sem("turned")
        xnT_ready = sem("xnT_ready")
        logits_done = sem("logits_done")
        logT_ready = sem("logT_ready")
        logits_turned = sem("logits_turned")
        xn_stored = sems("xn_stored", XB)
        gap_done = sem("gap_done")
        exp_gap = sem("exp_gap")
        counts_done = sem("counts_done")
        lo_ready = sem("lo_ready")
        lo_act = sem("lo_act")
        hi_known = sem("hi_known")
        hi_step = sem("hi_step")
        hi_ready = sems("hi_ready", 2)
        slots_known = sem("slots_known")
        lo_used = sem("lo_used")
        tokens_copied = sem("tokens_copied")
        inverse_done = sem("inverse_done")
        gathered = sems("gathered", 4)
        w_loaded = sems("w_loaded", 2)
        xT_ready = sem("xT_ready")
        xh_ready = sem("xh_ready")
        xl_ready = sem("xl_ready")
        h_ready = sems("h_ready", HC)
        hf_ready = sems("hf_ready", HC)
        hh_ready = sems("hh_ready", HC)
        hl_ready = sems("hl_ready", HC)
        yT_ready = sem("yT_ready")
        ytr_ready = sem("ytr_ready")
        y_ready = sem("y_ready")
        y_stored = sems("y_stored", 2)
        yg_in = sems("yg_in", 4)
        yg_used = sems("yg_used", 2)
        out_stored = sems("out_stored", 2)

        def row_scalars(ch, dve, t0, t1, others=iter(())):
            ts = slice(t0, t1)
            st, v, half, y, a = stats[:, ts], *(nw[:, q, ts] for q in range(4))

            def then(ins):
                ch.add(ins)
                done = ch.n
                next(others, None)
                ch.wait(done)

            ch.wait()
            ch.add(dve.tensor_tensor(a, st[:, :, 1], st[:, :, 4], ALU.subtract))
            ch.add(dve.tensor_tensor(y, st[:, :, 2], st[:, :, 5], ALU.add))
            then(dve.tensor_tensor(half, st[:, :, 1], st[:, :, 4], ALU.add))
            ch.add(dve.tensor_tensor(a, a, a, ALU.mult))
            then(dve.tensor_scalar(mean[:, ts], half, 0.5, None, ALU.mult))
            then(dve.scalar_tensor_tensor(a, a, C / 4, y, ALU.mult, ALU.add))
            then(dve.tensor_scalar(a, a, 1.0 / C, None, ALU.mult))
            ch.add(dve.tensor_scalar(v, a, EPS, None, ALU.add))
            then(dve.tensor_scalar(half, a, -0.5, -0.5 * EPS, ALU.mult, ALU.add))
            then(dve.tensor_scalar(y.bitcast(I32), v.bitcast(I32), -0.5, RSQRT_SEED, ALU.mult, ALU.add))
            for turn in range(3):
                then(dve.tensor_tensor(a, y, y, ALU.mult))
                then(dve.tensor_tensor(a, a, half, ALU.mult))
                then(dve.scalar_tensor_tensor(rstd[:, ts] if turn == 2 else y, a, 1.5, y, ALU.add, ALU.mult))
            dve.scalar_tensor_tensor(nmr[:, ts], mean[:, ts], -1.0, rstd[:, ts], ALU.mult, ALU.mult).then_inc(rstd_done, 1)

        def row_statistics(ch, dve, groups):
            for g in groups:
                dve.wait_ge(x_arrived[g % 4], 16 * (g // 4 + 1))
                for t in range(GT * g, GT * g + GT):
                    ch.add(dve.bn_stats(stats[:, t], x_sb[:, t]))
                    yield

        NBIAS = E * HC + E + 1

        def turn_bank(g):
            return bank[0] if g % 2 == 0 else bank[1]

        def transpose_weights(pe):
            pe.wait_ge(small_in[0], 64)
            for j in range(4):
                nc.tensor.transpose(bank[4][:, j * P:(j + 1) * P], wraw[:, j], ident[:])
            pe.wait_ge(small_in[1], 16 * 6)
            nc.tensor.transpose(bank[5][:, 0:NBIAS], brows[:], ident[0:NBIAS, 0:NBIAS]).then_inc(WT_ps, 1)

        PARTS = (0, NG // 2, NG)

        def logit_bank(g):
            return bank[2] if g < PARTS[1] else bank[6]

        def bias_pairs(dve, ch):
            dve.wait_ge(small_in[1], 16 * 6)
            ch.then(dve.tensor_copy(bhi[:], brow[:]))
            ch.add(dve.tensor_tensor(blo[:], brow[:], bhi[:].bitcast(F32), ALU.subtract))
            ch.then(dve.tensor_scalar(bsum[:], bhi[:].bitcast(F32), part01[:, 0:1], None, ALU.mult))
            ch.then(dve.scalar_tensor_tensor(bpair[:], blo[:].bitcast(F32), part01[:, 1:2], bsum[:], ALU.mult, ALU.add))

        class Route:

            def __init__(self, f, stage):
                self.f = f
                new = lambda name, shape, dt=F32: scoped(stage, f"{name}_{f}", shape, dt)
                self.L = new("logits", [P, NT, E])
                self.w = new("ranked", [P, NT, E])
                self.m = new("first", [P, NT])
                self.m2 = new("second", [P, NT])
                self.top = new("top", [P, NT])
                self.gap = new("gap", [P, NT])
                self.e2 = new("exp_gap_sb", [P, NT])
                self.choice = new("choice", [P, E, K, NT], BF16)
                self.pos = new("pos", [P, E, K * NT])
                self.cum = new("cum", [P, E, K * NT])
                self.base = new("base", [P, K * NT])
                self.at = new("at", [P, K * NT])
                self.at_i = new("at_i", [P, K * NT], I32)
                self.valid = new("valid", [P, K * NT])
                self.slotf = new("slotf", [P, K * NT])
                self.lof = new("lof", [P, K * NT])
                self.hif = new("hif", [P, K * NT])
                self.hi_oh = new("hi_oh", [P, K * NT, NCH])
                self.hi_tok = new("hi_tok", [P, K * NT, E * NCH], F32R)
                self.lo = new("lo", [P, 2, 16, P], F32R)
                self.away = new("away", [P, 2, 16 - LD, P])
                self.nlof = new("nlof", [P, K * NT])
                self.tok = new("tok", [E * NCH, P])
                self.xns = new("xns", [P, XB, GT, C])
                self.xnT = new("xnT", [P, 2, SEQ])
                self.logT = new("logT", [E, 2, SEQ])

            def sync(self, sp):
                f = self.f
                for g in range(NG):
                    sp.wait_ge(norm_dve, NG * f + g + 1)
                    sp.wait_ge(norm_act, NG * f + g + 1)
                    sp.dma_start(rows(xn_dram, g * SEQ), self.xns[:, g % XB]).then_inc(xn_stored[g % XB], 16)
                    if f == 0 and g >= RB:
                        sp.wait_ge(exp_lo, g - RB + 1)
                        load_expert(sp, g)
                for e in range(2):
                    if f == 0:
                        sp.wait_ge(exp_lo, e + 1)
                    sp.dma_start(wst[e][:].bitcast(F32), wres[:, e].bitcast(F32)).then_inc(w_loaded[e], 16)
                    if f == 0:
                        sp.wait_ge(WT_sb, 2)
                    sp.dma_start(bst[e][:], bcol[:, e * (HC + 1):(e + 1) * (HC + 1)]).then_inc(w_loaded[e], 16)
                for u in range(XB):
                    sp.wait_ge(xn_stored[u], 16 * NG // XB * (f + 1))
                for e in range(2):
                    sp.wait_ge(w_loaded[e], 32 * (E // 2 * f + 1))

            def buffer_free(self, eng, g):
                G = NG * self.f + g
                if g >= XB:
                    eng.wait_ge(xn_stored[g % XB], 16 * (G // XB))
                    eng.wait_ge(turned, G - XB + 1)

            def scalar_norm(self, act, between=lambda g: None):
                f = self.f

                def norm(g):
                    act.wait_ge(rstd_done, 2 * f + (1 if g < EARLY[f] else 2))
                    self.buffer_free(act, g)
                    t = GT * g + GT - 1
                    nc.scalar.activation(self.xns[:, g % XB, GT - 1], x_sb[:, t], ACT.Identity,
                                         bias=nmr[:, t:t + 1], scale=rstd[:, t:t + 1]).then_inc(norm_act, 1)

                def xnT_out(g):
                    act.wait_ge(turned, NG * f + g + 1)
                    if g >= 2:
                        act.wait_ge(logits_done, NG * f + g - 1)
                    nc.scalar.copy(self.xnT[:, g % 2], turn_bank(g)[:]).then_inc(xnT_ready, 1)

                def logT_out(g):
                    act.wait_ge(logits_done, NG * f + g + 1)
                    if g >= 2:
                        act.wait_ge(logits_turned, NG * f + g - 1)
                    nc.scalar.copy(self.logT[:, g % 2], bank[3 + g % 2][0:E]).then_inc(logT_ready, 1)

                norm(0)
                norm(1)
                for g in range(NG):
                    if g + 2 < NG:
                        norm(g + 2)
                    xnT_out(g)
                    if g >= 1:
                        logT_out(g - 1)
                    between(g)
                logT_out(NG - 1)

            def scalar_gate(self, act):
                act.wait_ge(gap_done, self.f + 1)
                nc.scalar.activation(self.e2[:], self.gap[:], ACT.Exp).then_inc(exp_gap, 1)

            def tensor(self, pe):
                f = self.f

                def turn(g):
                    pe.wait_ge(norm_dve, NG * f + g + 1)
                    pe.wait_ge(norm_act, NG * f + g + 1)
                    if g >= 2:
                        pe.wait_ge(xnT_ready, NG * f + g - 1)
                    for t in range(GT):
                        last = nc.tensor.transpose(turn_bank(g)[:, t * P:(t + 1) * P], self.xns[:, g % XB, t], ident[:])
                    last.then_inc(turned, 1)

                def logits(g):
                    pe.wait_ge(xnT_ready, NG * f + g + 1)
                    if g >= 2:
                        pe.wait_ge(logT_ready, NG * f + g - 1)
                    nc.tensor.matmul(bank[3 + g % 2][0:E], wg_sb[:], self.xnT[:, g % 2], start=True, stop=True).then_inc(logits_done, 1)

                def logits_back(g):
                    pe.wait_ge(logT_ready, NG * f + g + 1)
                    for t in range(GT * g, GT * g + GT):
                        last = nc.tensor.transpose(logit_bank(g)[:, t * E:(t + 1) * E], self.logT[:, g % 2, (t % GT) * P:(t % GT + 1) * P], ident[0:E, 0:E])
                    last.then_inc(logits_turned, 1)

                turn(0)
                for g in range(NG):
                    if g + 1 < NG:
                        turn(g + 1)
                    logits(g)
                    if g >= 1:
                        logits_back(g - 1)
                logits_back(NG - 1)
                if f == 0:
                    transpose_weights(pe)
                if f == 0:
                    pe.wait_ge(WT_sb, 2)
                pe.wait_ge(gap_done, f + 1)
                flat = self.choice[:].rearrange("p e k t -> p (e k t)")
                nc.tensor.matmul(bank[3][:], tri[:], flat, start=True, stop=True)
                nc.tensor.matmul(bank[4][:], ones_bf[:], flat, start=True, stop=True).then_inc(counts_done, 1)
                for q in range(4):
                    Q = 4 * f + q
                    pe.wait_ge(hi_ready[min(q, 1)], f + 1 if q == 0 else 3 * f + q)
                    for j in range(16):
                        if j == 0:
                            pe.wait_ge(lo_ready, Q + 1)
                        elif j == LD:
                            pe.wait_ge(lo_act, Q + 1)
                        last = nc.tensor.matmul(bank[5][0:E * NCH, 0:P], self.hi_tok[:, 16 * q + j], self.lo[:, q % 2, j],
                                                start=(q == 0 and j == 0), stop=(q == 3 and j == 15))
                    last.then_inc(lo_used, 1)
                pe.wait_ge(tokens_copied, f + 1)
                nc.tensor.transpose(bank[0][:, 0:E * NCH], self.tok[:], ident[0:E * NCH, 0:E * NCH]).then_inc(inverse_done, 1)

            def gpsimd_columns(self, gp):
                f = self.f
                gp.wait_ge(hi_known, f + 1)
                for k in range(K):
                    mine = self.hi_oh[:, k * NT:(k + 1) * NT]
                    nc.gpsimd.tensor_tensor(mine, mine, token_id[:].unsqueeze(2).to_broadcast([P, NT, NCH]), ALU.mult).then_inc(hi_step, 1)
                gp.wait_ge(hi_step, K * (f + 1))
                for q in range(1, 4):
                    self.expert_columns(gp, q)

            def expert_columns(self, eng, q):
                js = slice(16 * q, 16 * q + 16)
                by_pair = self.choice[:].rearrange("p e k t -> p (k t) e")
                eng.tensor_tensor(self.hi_tok[:, js].rearrange("p j (e h) -> p j e h", e=E),
                                  by_pair[:, js].unsqueeze(3).to_broadcast([P, 16, E, NCH]),
                                  self.hi_oh[:, js].unsqueeze(2).to_broadcast([P, 16, E, NCH]), ALU.mult).then_inc(hi_ready[min(q, 1)], 1)

            def scalar_rows(self, act, ch):
                f = self.f
                act.wait_ge(slots_known, f + 1)
                for q in range(4):
                    Q = 4 * f + q
                    for j in range(16 - LD):
                        at = 16 * q + LD + j
                        ch.add(nc.scalar.activation(self.away[:, q % 2, j], iota_lo[:], ACT.Abs, bias=self.nlof[:, at:at + 1]))
                    ch.wait()
                    if Q >= 2:
                        act.wait_ge(lo_used, Q - 1)
                    nc.scalar.activation(self.lo[:, q % 2, LD:], self.away[:, q % 2], ACT.Relu, bias=1.0, scale=-1.0).then_inc(lo_act, 1)

            def top2(self, dve, ch, part):
                ts = slice(GT * PARTS[part], GT * PARTS[part + 1])
                n = ts.stop - ts.start
                L, w, top = self.L[:, ts], self.w[:, ts], self.top[:, ts]
                bt = lambda a: a.unsqueeze(2).to_broadcast([P, n, E])
                oh = [self.choice[:, :, k, ts].rearrange("p e t -> p t e") for k in range(K)]
                logits = logit_bank(PARTS[part])[:, ts.start * E:ts.stop * E].rearrange("p (t e) -> p t e", e=E)
                for k in range(K):
                    rest = logits if k == 0 else L
                    mk = (self.m if k == 0 else self.m2)[:, ts]
                    ch.then(dve.tensor_reduce(mk, rest, AX, ALU.max))
                    ch.then(dve.tensor_tensor(w, rest, bt(mk), ALU.is_equal))
                    ch.then(dve.tensor_tensor(w, w, prefer[:].unsqueeze(1).to_broadcast([P, n, E]), ALU.mult))
                    ch.then(dve.tensor_reduce(top, w, AX, ALU.max))
                    ch.then(dve.tensor_tensor(oh[k], w, bt(top), ALU.is_equal))
                    if k == 0:
                        ch.then(dve.scalar_tensor_tensor(L, oh[0], FAR, logits, ALU.mult, ALU.add))

            def vector(self, dve, ch):
                f = self.f
                for g in range(NG):
                    if g == 3:
                        row_scalars(ch, dve, GT * EARLY[f], NT)
                    self.buffer_free(dve, g)
                    for t in range(GT * g, GT * g + GT - 1):
                        last = dve.tensor_scalar(self.xns[:, g % XB, t % GT], x_sb[:, t], mean[:, t:t + 1], rstd[:, t:t + 1], ALU.subtract, ALU.mult)
                    last.then_inc(norm_dve, 1)
                if f == 0:
                    dve.wait_ge(consts, 1)
                for part in range(len(PARTS) - 1):
                    dve.wait_ge(logits_turned, NG * f + PARTS[part + 1])
                    self.top2(dve, ch, part)
                    if f == 0 and part == 0:
                        bias_pairs(dve, ch)
                m, m2, gap, e2, choice = self.m, self.m2, self.gap, self.e2, self.choice
                dve.tensor_tensor(gap[:], m2[:], m[:], ALU.subtract).then_inc(gap_done, 1)
                ek = lambda a: a.unsqueeze(2).to_broadcast([P, E, K * NT])
                ch2 = choice[:].rearrange("p e k t -> p e (k t)")
                by_tok = lambda a: a.rearrange("p e j -> p j e")
                ch.add(dve.memset(self.cum[:, 0, 0:1], 0.0))
                ch.then(dve.tensor_tensor(self.pos[:], ch2, ek(expert_base[:]), ALU.mult))
                ch.then(dve.tensor_reduce(self.base[:], by_tok(self.pos[:]), AX, ALU.add))
                dve.wait_ge(counts_done, f + 1)
                fl = lambda a: a.rearrange("p e j -> p (e j)")
                ch.then(dve.tensor_tensor_scan(fl(self.cum[:])[:, 1:], bank[4][:, 0:E * K * NT - 1], fl(carry[:])[:, 1:], 0.0, ALU.add, ALU.mult))
                ch.then(dve.scalar_tensor_tensor(fl(self.cum[:]), bank[3][:], -1.0, fl(self.cum[:]), ALU.add, ALU.add))
                ch.then(dve.tensor_tensor(self.pos[:], self.cum[:], ch2, ALU.mult))
                ch.then(dve.tensor_reduce(self.at[:], by_tok(self.pos[:]), AX, ALU.add))
                ch.then(dve.tensor_copy(self.at_i[:], self.at[:]))
                ch.then(dve.tensor_scalar(self.at_i[:], self.at_i[:], P - 1, None, ALU.bitwise_and))
                ch.then(dve.tensor_copy(self.lof[:], self.at_i[:]))
                ch.then(dve.tensor_tensor(self.hif[:], self.at[:], self.lof[:], ALU.subtract))
                dve.tensor_scalar(self.nlof[:], self.lof[:], -1.0, None, ALU.mult).then_inc(slots_known, 1)
                dve.tensor_tensor(self.hi_oh[:], self.hif[:].unsqueeze(2).to_broadcast([P, K * NT, NCH]),
                                  iota_hi[:].unsqueeze(1).to_broadcast([P, K * NT, NCH]), ALU.is_equal).then_inc(hi_known, 1)
                for q in range(4):
                    Q = 4 * f + q
                    if Q >= 2:
                        dve.wait_ge(lo_used, Q - 1)
                    dve.tensor_tensor(self.lo[:, q % 2, 0:LD], iota_lo[:].unsqueeze(1).to_broadcast([P, LD, P]),
                                      self.lof[:, 16 * q:16 * q + LD].unsqueeze(2).to_broadcast([P, LD, P]), ALU.is_equal).then_inc(lo_ready, 1)
                    if q == 0:
                        dve.wait_ge(hi_step, K * f + 1)
                        self.expert_columns(dve, 0)
                ch.then(dve.tensor_scalar(self.valid[:], self.at[:], float(CAP), None, ALU.is_lt))
                ch.then(dve.tensor_tensor(self.slotf[:], self.at[:], self.valid[:], ALU.mult))
                ch.then(dve.tensor_tensor(slot[:].rearrange("p k t -> p (k t)"), self.slotf[:], self.base[:], ALU.add))
                dve.wait_ge(exp_gap, f + 1)
                gf = lambda k: gate[:, k]
                ch.then(dve.tensor_scalar(self.top[:], e2[:], 1.0, None, ALU.add))
                ch.then(dve.reciprocal(gap[:], self.top[:]))
                dve.wait_ge(lo_used, 4 * (f + 1))
                dve.tensor_copy(self.tok[:], bank[5][0:E * NCH, 0:P]).then_inc(tokens_copied, 1)
                vk = lambda k: self.valid[:, k * NT:(k + 1) * NT]
                ch.add(dve.scalar_tensor_tensor(gf(0), gap[:], 0.5, vk(0), ALU.mult, ALU.mult))
                ch.then(dve.tensor_tensor(e2[:], e2[:], gap[:], ALU.mult))
                ch.then(dve.scalar_tensor_tensor(gf(1), e2[:], 0.5, vk(1), ALU.mult, ALU.mult))
                dve.wait_ge(inverse_done, f + 1)
                ch.then(dve.tensor_copy(gidx[:], bank[0][:, 0:E * NCH]))

        class Experts:

            def __init__(self, f, stage):
                self.f, self.b = f, NSB * f
                new = lambda name, shape, dt=F32: scoped(stage, f"{name}_{f}", shape, dt)
                self.xg = new("xg", [P, 4, GT, C])
                self.xh = new("xh", [P, 2, 512], F32R)
                self.xl = new("xl", [P, 2, 512], F32R)
                self.hf = new("hf", [P, HC, 512])
                self.hh = new("hh", [P, 2, HC, 512], F32R)
                self.hl = new("hl", [P, 2, HC, 512], F32R)
                self.yT = new("yT", [P, 512])
                self.y_sb = new("y_sb", [P, 2, GT, C])

            def schedule(self, eng, step):
                step(0, 0)
                step(0, 1)
                if self.f == 0:
                    for r in range(2, 6):
                        step(0, r)
                with eng.Fori(1 if self.f == 0 else 0, 3) as i:
                    for r in range(2, 6):
                        step(i, r)
                for r in range(2, 6):
                    step(3, r)

            @staticmethod
            def has(i, r, d):
                if isinstance(i, int):
                    return 0 <= 4 * i + r - d < NSB
                return True

            def sync(self, sp):
                def step(i, r):
                    s = 4 * i + r
                    if self.has(i, r, 2):
                        sp.wait_ge(y_ready, self.b + s - 1)
                        sp.dma_start(rows(y_dram, (s - 2) * 512), self.y_sb[:, r % 2]).then_inc(y_stored[r % 2], 16)
                    if r % 2 == 0 and not (isinstance(i, int) and (s < 2 or s + 2 >= NSB)):
                        slot_ = (r // 2 + 1) % 2
                        sp.wait_ge(hl_free, self.b + s)
                        sp.dma_start(wst[slot_][:].bitcast(F32), wres[:, bass.ds(2 * i + r // 2 + 1, 1)].rearrange("p a w n -> p (a w) n").bitcast(F32)).then_inc(w_loaded[slot_], 16)
                        sp.wait_ge(yT_ready, self.b + s)
                        sp.dma_start(bst[slot_][:], bcol[:, bass.ds((2 * i + r // 2 + 1) * (HC + 1), HC + 1)]).then_inc(w_loaded[slot_], 16)
                self.schedule(sp, step)
                for u in range(2):
                    sp.wait_ge(y_stored[u], 16 * NSB // 2 * (self.f + 1))

            def gpsimd(self, gp):
                for s in range(NSB):
                    S = self.b + s
                    if S >= 4:
                        gp.wait_ge(xT_ready, S - 3)
                    for t in range(GT):
                        j = GT * s + t
                        gp.indirect_dma_start(out=self.xg[:, s % 4, t], out_offset=None, in_=xn_dram,
                                              in_offset=bass.IndirectOffsetOnAxis(ap=gidx[:, j:j + 1], axis=0)).then_inc(gathered[s % 4], 16)

            def tensor(self, pe):
                f, b = self.f, self.b

                def turn(i, r):
                    pe.wait_ge(gathered[r % 4], 64 * (4 * f + i + r // 4 + 1))
                    if not (isinstance(i, int) and b + 4 * i + r == 0):
                        pe.wait_ge(xl_ready, b + 4 * i + r)
                    for t in range(GT):
                        last = nc.tensor.transpose(bank[0][:, t * P:(t + 1) * P], self.xg[:, r % 4, t], ident[:])
                    last.then_inc(xT_ready, 1)

                def up(i, r, c):
                    w = wst[(r // 2) % 2]
                    s = 4 * i + r
                    if c == 0:
                        pe.wait_ge(xl_ready, b + s + 1)
                        pe.wait_ge(w_loaded[(r // 2) % 2], 32 * (4 * f + i + r // 4 + 1))
                    pe.wait_ge(hf_ready[c], b + s)
                    at = slice(c * P, (c + 1) * P)
                    nc.tensor.matmul(bank[1 + c][:], w[:, 0, at], self.xh[:, r % 2], start=True, stop=False)
                    nc.tensor.matmul(bank[1 + c][:], w[:, 0, at], self.xl[:, r % 2], start=False, stop=False)
                    nc.tensor.matmul(bank[1 + c][:], w[:, 2, at], self.xh[:, r % 2], start=False, stop=True).then_inc(h_ready[c], 1)

                def down(i, r, c):
                    w = wst[(r // 2) % 2]
                    s = 4 * i + r
                    pe.wait_ge(hl_ready[c], b + s + 1)
                    sums = bank[5 + 2 * (r % 2)]
                    if c == 0 and not (isinstance(i, int) and b + s < 2):
                        pe.wait_ge(yT_ready, b + s - 1)
                    at = slice(c * P, (c + 1) * P)
                    nc.tensor.matmul(sums[:], w[:, 1, at], self.hh[:, r % 2, c], start=(c == 0), stop=False)
                    nc.tensor.matmul(sums[:], w[:, 1, at], self.hl[:, r % 2, c], start=False, stop=False)
                    last = nc.tensor.matmul(sums[:], w[:, 3, at], self.hh[:, r % 2, c], start=False, stop=(c == HC - 1))
                    if c == HC - 1:
                        last.then_inc(hl_free, 1)

                def back(i, r):
                    s = 4 * i + r
                    pe.wait_ge(yT_ready, b + s + 1)
                    pe.wait_ge(y_ready, b + s)
                    for t in range(GT):
                        last = nc.tensor.transpose(bank[6][:, t * P:(t + 1) * P], self.yT[:, t * P:(t + 1) * P], ident[:])
                    last.then_inc(ytr_ready, 1)

                def step(i, r):
                    for c in range(HC):
                        if self.has(i, r, 0):
                            up(i, r, c)
                        if c == 1 and self.has(i, r, 2):
                            back(i, r - 2)
                        if self.has(i, r, 1):
                            down(i, r - 1, c)
                        if c == 0 and self.has(i, r, -1):
                            turn(i, r + 1)
                turn(0, 0)
                self.schedule(pe, step)

            def scalar(self, act):
                f, b = self.f, self.b

                def high(i, r):
                    act.wait_ge(xT_ready, b + 4 * i + r + 1)
                    nc.scalar.copy(self.xh[:, r % 2], bank[0][:]).then_inc(xh_ready, 1)

                def step(i, r):
                    s = 4 * i + r
                    if self.has(i, r, 2):
                        act.wait_ge(hl_free, b + s - 1)
                        act.wait_ge(ytr_ready, b + s - 2)
                        nc.scalar.activation(self.yT[:], bank[5 + 2 * (r % 2)][:], ACT.Identity,
                                             bias=bst[(r // 2 + 1) % 2][:, HC:HC + 1]).then_inc(yT_ready, 1)
                    for c in range(HC):
                        if self.has(i, r, 0):
                            act.wait_ge(h_ready[c], b + s + 1)
                            act.wait_ge(hl_ready[c], b + s)
                            bias = bst[(r // 2) % 2][:, c:c + 1]
                            one = nc.scalar.activation(self.hf[:, c], bank[1 + c][:], ACT.Relu, bias=bias)
                            if c == HC - 1:
                                one = nc.scalar.activation(self.hh[:, r % 2, c], bank[1 + c][:], ACT.Relu, bias=bias)
                            one.then_inc(hf_ready[c], 1)
                        if c == 0 and self.has(i, r, -1):
                            high(i, r + 1)
                high(0, 0)
                self.schedule(act, step)

            def vector(self, dve):
                f, b = self.f, self.b

                def low(i, r):
                    dve.wait_ge(xh_ready, b + 4 * i + r + 1)
                    dve.tensor_tensor(self.xl[:, r % 2], bank[0][:], self.xh[:, r % 2].bitcast(F32), ALU.subtract).then_inc(xl_ready, 1)

                def step(i, r):
                    s = 4 * i + r
                    here = self.has(i, r, 0)

                    def h_high(c):
                        dve.wait_ge(hf_ready[c], b + s + 1)
                        dve.tensor_copy(self.hh[:, r % 2, c], self.hf[:, c]).then_inc(hh_ready[c], 1)

                    def h_low(c):
                        if c < HC - 1:
                            dve.wait_ge(hh_ready[c], b + s + 1)
                        else:
                            dve.wait_ge(hf_ready[c], b + s + 1)
                        dve.tensor_tensor(self.hl[:, r % 2, c], self.hf[:, c], self.hh[:, r % 2, c].bitcast(F32), ALU.subtract).then_inc(hl_ready[c], 1)
                    if here:
                        h_high(0)
                    if self.has(i, r, 2):
                        u = r % 2
                        dve.wait_ge(ytr_ready, b + s - 1)
                        dve.wait_ge(y_stored[u], 16 * (8 * f + 2 * i + (r - 2) // 2))
                        dve.tensor_copy(self.y_sb[:, u].rearrange("p t c -> p (t c)"), bank[6][:]).then_inc(y_ready, 1)
                    if here:
                        h_low(0)
                    if self.has(i, r, -1):
                        low(i, r + 1)
                    if here:
                        h_high(1)
                        h_low(1)
                        h_high(2)
                        h_low(2)
                        h_low(3)
                low(0, 0)
                self.schedule(dve, step)

        hl_free = sem("hl_free")

        ones_col = sem("ones_col")
        an_stats = sem("an_stats")
        an_scale = sem("an_scale")
        an_ready = sem("an_ready")
        an_turned = sem("an_turned")
        anT_ready = sem("anT_ready")
        q_ready = sem("q_ready")
        q_split = sem("q_split")
        q_parts = sem("q_parts")
        qT_ready = sem("qT_ready")
        kv_ready = sem("kv_ready")
        k_split = sem("k_split")
        k_parts = sem("k_parts")
        v_copied = sem("v_copied")
        k_rows = sem("k_rows")
        keysum_ready = sem("keysum_ready")
        kv_masked = sem("kv_masked")
        num_ready = sem("num_ready")
        den_step = sem("den_step")
        att_ready = sem("att_ready")
        att_turned = sem("att_turned")
        attT_ready = sem("attT_ready")
        o_ready = sem("o_ready")
        x_summed = sem("x_summed")

        class Gather:

            def __init__(self, stage, f):
                self.f = f
                self.yg = scoped(stage, f"yg_{f}", [P, 2, K, GT, C])

            def gpsimd(self, gp):
                f = self.f
                for n in range(NG):
                    u = n % 2
                    for k in range(K):
                        if f * NG + n >= 2:
                            gp.wait_ge(yg_used[k], NG * f + n - 1)
                        for t in range(GT):
                            gp.indirect_dma_start(out=self.yg[:, u, k, t], out_offset=None, in_=y_dram,
                                                  in_offset=bass.IndirectOffsetOnAxis(ap=slot[:, k, GT * n + t:GT * n + t + 1], axis=0)).then_inc(yg_in[2 * u + k], 16)

        class Attention:

            STEPS = NG + 3

            def __init__(self, stage, gather):
                new = lambda name, shape: scoped(stage, name, shape)
                self.yg = gather.yg
                self.an = new("an", [P, 2, GT, C])
                self.anT = new("anT", [P, 2, SEQ])
                self.qe = new("qe", [P, 2, SEQ])
                self.qr = new("qr", [P, 2, SEQ])
                self.ke = new("ke", [P, 2, SEQ])
                self.kr = new("kr", [P, 2, SEQ])
                self.qT = new("qT", [P, 2, SEQ])
                self.kk = new("kk", [P, 2, GT, C])
                self.vv = new("vv", [P, 2, GT, C + 1])
                self.kv = new("kv", [P, 2, C + HEADS])
                self.den = new("den", [P, 2, GT, HEADS])
                self.att = new("att", [P, 2, GT, C])
                self.attT = new("attT", [P, 2, SEQ])
                self.sta = new("sta", [P, 2, GT, 6])
                self.agg = new("agg", [P, 2, GT, 2])
                self.nwa = new("nwa", [P, 2, 3, GT])
                self.rsa = new("rsa", [P, 2, 2, GT])

            def tensor(self, pe):
                def turn_out(n):
                    pe.wait_ge(att_ready, n + 1)
                    if n >= 1:
                        pe.wait_ge(attT_ready, n)
                    for t in range(GT):
                        last = nc.tensor.transpose(bank[6][:, t * P:(t + 1) * P], self.att[:, n % 2, t], ident[:])
                    last.then_inc(att_turned, 1)

                def turn(n):
                    pe.wait_ge(an_ready, n + 1)
                    if n >= 1:
                        pe.wait_ge(anT_ready, n)
                    for t in range(GT):
                        last = nc.tensor.transpose(bank[0][:, t * P:(t + 1) * P], self.an[:, n % 2, t], ident[:])
                    last.then_inc(an_turned, 1)

                def project(n):
                    pe.wait_ge(attT_ready, n + 1)
                    if n >= 1:
                        pe.wait_ge(x_summed, n)
                    for t in range(GT):
                        at = slice(t * P, (t + 1) * P)
                        nc.tensor.matmul(bank[7][:, at], self.attT[:, n % 2, at], WT[:, 3], start=True, stop=False)
                        last = nc.tensor.matmul(bank[7][:, at], ones2[:], bpair[:, 2], start=False, stop=True)
                    last.then_inc(o_ready, 1)

                def keysum(n):
                    pe.wait_ge(k_rows, n + 1)
                    pe.wait_ge(v_copied, n + 1)
                    if n == 0:
                        pe.wait_ge(ones_col, 1)
                    else:
                        pe.wait_ge(att_ready, n)
                    for t in range(GT):
                        last = nc.tensor.matmul(bank[4][:, 0:C + 1], self.kk[:, n % 2, t], self.vv[:, n % 2, t], start=(t == 0), stop=(t == GT - 1))
                    last.then_inc(keysum_ready, 1)

                def q(n):
                    pe.wait_ge(anT_ready, n + 1)
                    if n >= 1:
                        pe.wait_ge(q_parts, n)
                    nc.tensor.matmul(bank[1][:], WT[:, 0], self.anT[:, n % 2], start=True, stop=True).then_inc(q_ready, 1)

                def query(n):
                    pe.wait_ge(kv_masked, 2 * n + 2)
                    pe.wait_ge(qT_ready, n + 1)
                    if n >= 1:
                        pe.wait_ge(att_ready, n)
                    for t in range(GT):
                        at = slice(t * P, (t + 1) * P)
                        nc.tensor.matmul(bank[5][:, at], self.qT[:, n % 2, at], self.kv[:, n % 2, 0:C], start=True, stop=True)
                        last = nc.tensor.matmul(bank[4][:, 256 + t * HEADS:256 + (t + 1) * HEADS], self.qT[:, n % 2, at],
                                                self.kv[:, n % 2, C:C + HEADS], start=True, stop=True)
                    last.then_inc(num_ready, 1)

                def kv(n):
                    if n >= 1:
                        pe.wait_ge(k_parts, n)
                        pe.wait_ge(v_copied, n)
                    for w in (0, 1):
                        for t in range(GT):
                            at = slice(t * P, (t + 1) * P)
                            nc.tensor.matmul(bank[2 + w][:, at], self.anT[:, n % 2, at], WT[:, 1 + w], start=True, stop=False)
                            last = nc.tensor.matmul(bank[2 + w][:, at], ones2[:], bpair[:, w], start=False, stop=True)
                        last.then_inc(kv_ready, 1)

                for s in range(self.STEPS):
                    middle, late = 2 <= s <= NG + 1, 3 <= s <= NG + 2
                    if 1 <= s <= NG:
                        turn(s - 1)
                    if late and s <= NG:
                        turn_out(s - 3)
                    if 1 <= s <= NG:
                        q(s - 1)
                    if middle:
                        keysum(s - 2)
                    if late and s > NG:
                        turn_out(s - 3)
                    if 1 <= s <= NG:
                        kv(s - 1)
                    if middle:
                        query(s - 2)
                    if late:
                        project(s - 3)

            def scalar(self, act):
                def attT_out(n):
                    act.wait_ge(att_turned, n + 1)
                    if n >= 2:
                        act.wait_ge(o_ready, n - 1)
                    nc.scalar.copy(self.attT[:, n % 2], bank[6][:]).then_inc(attT_ready, 1)

                def norm(n):
                    act.wait_ge(an_scale, n + 1)
                    if n >= 2:
                        act.wait_ge(an_turned, n - 1)
                    for t in range(GT):
                        last = nc.scalar.activation(self.an[:, n % 2, t], x_sb[:, GT * n + t], ACT.Identity,
                                                    bias=self.rsa[:, n % 2, 1, t:t + 1], scale=self.rsa[:, n % 2, 0, t:t + 1])
                    last.then_inc(an_ready, 1)

                def anT_out(n):
                    act.wait_ge(an_turned, n + 1)
                    if n >= 2:
                        act.wait_ge(kv_ready, 2 * (n - 1))
                    nc.scalar.copy(self.anT[:, n % 2], bank[0][:]).then_inc(anT_ready, 1)

                def q_act(n):
                    u = n % 2
                    act.wait_ge(q_ready, n + 1)
                    if n >= 2:
                        act.wait_ge(qT_ready, n - 1)
                    nc.scalar.activation(self.qe[:, u], bank[1][:], ACT.Relu, bias=nbq[:], scale=-1.0).then_inc(q_split, 1)
                    nc.scalar.activation(self.qr[:, u], bank[1][:], ACT.Relu, bias=bcol[:, NBIAS - 1:NBIAS])
                    act.wait_ge(q_split, n + 1)
                    nc.scalar.activation(self.qe[:, u], self.qe[:, u], ACT.Exp, scale=-1.0).then_inc(q_parts, 1)

                def k_act(n):
                    u = n % 2
                    act.wait_ge(kv_ready, 2 * n + 1)
                    if n >= 2:
                        act.wait_ge(k_rows, n - 1)
                    nc.scalar.activation(self.ke[:, u], bank[2][:], ACT.Relu, scale=-1.0).then_inc(k_split, 1)
                    nc.scalar.activation(self.kr[:, u], bank[2][:], ACT.Relu)
                    act.wait_ge(k_split, n + 1)
                    nc.scalar.activation(self.ke[:, u], self.ke[:, u], ACT.Exp, scale=-1.0).then_inc(k_parts, 1)

                def v_out(n):
                    act.wait_ge(kv_ready, 2 * n + 2)
                    if n >= 2:
                        act.wait_ge(keysum_ready, n - 1)
                    nc.scalar.copy(self.vv[:, n % 2, :, 0:C], bank[3][:].rearrange("p (t c) -> p t c", c=C)).then_inc(v_copied, 1)

                for s in range(self.STEPS):
                    if 1 <= s <= NG:
                        norm(s - 1)
                        anT_out(s - 1)
                        q_act(s - 1)
                    if 3 <= s <= NG + 2:
                        attT_out(s - 3)
                    if 1 <= s <= NG:
                        k_act(s - 1)
                        v_out(s - 1)

            def vector(self, dve, ch):
                def add_rows(n, k, t):
                    if t == 0:
                        dve.wait_ge(yg_in[2 * (n % 2) + k], 64 * (n // 2 + 1))
                        if k == 1:
                            dve.wait_ge(yg_used[0], n + 1)
                    at = GT * n + t
                    one = dve.scalar_tensor_tensor(x_sb[:, at], self.yg[:, n % 2, k, t], gate[:, k, at:at + 1], x_sb[:, at], ALU.mult, ALU.add)
                    if t == GT - 1:
                        one.then_inc(yg_used[k], 1)

                def an_statistics(n):
                    dve.wait_ge(yg_used[1], n + 1)
                    if n >= 2:
                        dve.wait_ge(an_ready, n - 1)
                    for t in range(GT):
                        last = dve.bn_stats(self.sta[:, n % 2, t], x_sb[:, GT * n + t])
                    last.then_inc(an_stats, 1)

                def scale_steps(n):
                    u = n % 2
                    v, y, a = (self.nwa[:, u, q] for q in range(3))
                    dve.wait_ge(an_stats, n + 1)
                    for t in range(GT):
                        ch.add(dve.bn_aggr(self.agg[:, u, t], self.sta[:, u, t]))
                    done = ch.n
                    yield
                    ch.wait(done)
                    ch.add(dve.tensor_scalar(v, self.agg[:, u, :, 1], EPS, None, ALU.add))
                    done = ch.n
                    yield
                    ch.wait(done)
                    ch.add(dve.tensor_scalar(y.bitcast(I32), v.bitcast(I32), -0.5, NEG_EIGHTH_SEED, ALU.mult, ALU.add))
                    done = ch.n
                    yield
                    for square in (64.0, 16.0, 4.0):
                        ch.wait(done)
                        ch.add(dve.scalar_tensor_tensor(a, y, square, y, ALU.mult, ALU.mult))
                        done = ch.n
                        yield
                        ch.wait(done)
                        ch.add(dve.tensor_tensor(a, a, v, ALU.mult))
                        done = ch.n
                        yield
                        ch.wait(done)
                        to = self.rsa[:, u, 0] if square == 4.0 else y
                        ch.add(dve.scalar_tensor_tensor(to, a, -3.0, y, ALU.add, ALU.mult))
                        done = ch.n
                        yield
                    ch.wait(done)
                    dve.scalar_tensor_tensor(self.rsa[:, u, 1], self.agg[:, u, :, 0], -1.0, self.rsa[:, u, 0], ALU.mult, ALU.mult).then_inc(an_scale, 1)
                    yield

                def k_sum(n):
                    dve.wait_ge(k_parts, n + 1)
                    if n >= 2:
                        dve.wait_ge(keysum_ready, n - 1)
                    dve.tensor_tensor(self.kk[:, n % 2].rearrange("p t c -> p (t c)"), self.ke[:, n % 2], self.kr[:, n % 2], ALU.add).then_inc(k_rows, 1)

                def q_sum(n):
                    dve.wait_ge(q_parts, n + 1)
                    if n >= 2:
                        dve.wait_ge(num_ready, n - 1)
                    dve.tensor_tensor(self.qT[:, n % 2], self.qe[:, n % 2], self.qr[:, n % 2], ALU.add).then_inc(qT_ready, 1)

                def kv_mask(n):
                    u = n % 2
                    dve.wait_ge(keysum_ready, n + 1)
                    if n >= 2:
                        dve.wait_ge(num_ready, n - 1)
                    dve.tensor_tensor(self.kv[:, u, 0:C], bank[4][:, 0:C], block_mask[:], ALU.mult).then_inc(kv_masked, 1)
                    dve.tensor_tensor(self.kv[:, u, C:C + HEADS], head_mask[:], bank[4][:, C:C + 1].to_broadcast([P, HEADS]), ALU.mult).then_inc(kv_masked, 1)

                def den_max(n):
                    dve.wait_ge(num_ready, n + 1)
                    dve.tensor_scalar(self.den[:, n % 2], bank[4][:, 256:256 + GT * HEADS].rearrange("p (t h) -> p t h", h=HEADS), 1e-6, None, ALU.max).then_inc(den_step, 1)

                def den_inverse(n):
                    dve.wait_ge(den_step, 2 * n + 1)
                    dve.reciprocal(self.den[:, n % 2], self.den[:, n % 2]).then_inc(den_step, 1)

                def divide(n):
                    u = n % 2
                    dve.wait_ge(den_step, 2 * n + 2)
                    if n >= 2:
                        dve.wait_ge(att_turned, n - 1)
                    dve.tensor_tensor(self.att[:, u].rearrange("p t (h d) -> p (t h) d", d=HD), bank[5][:].rearrange("p (a d) -> p a d", d=HD),
                                      self.den[:, u].rearrange("p t h -> p (t h)").unsqueeze(2).to_broadcast([P, GT * HEADS, HD]), ALU.mult).then_inc(att_ready, 1)

                def residual(n):
                    dve.wait_ge(o_ready, n + 1)
                    xb = x_sb[:, GT * n:GT * n + GT]
                    dve.tensor_tensor(xb, bank[7][:].rearrange("p (t c) -> p t c", c=C), xb, ALU.add).then_inc(x_summed, 1)

                def statistics(groups):
                    for n in groups:
                        dve.wait_ge(x_summed, n + 1)
                        for t in range(GT * n, GT * n + GT):
                            ch.add(dve.bn_stats(stats[:, t], x_sb[:, t]))
                            yield

                for k in range(K):
                    for t in range(GT):
                        add_rows(0, k, t)
                for s in range(self.STEPS):
                    front, middle = s < NG, 2 <= s <= NG + 1
                    if 2 <= s <= NG:
                        k_sum(s - 2)
                    if front:
                        an_statistics(s)
                    scale = scale_steps(s) if front else iter(())
                    next(scale, None)
                    if s == 0:
                        finish(scale)
                    for k in range(K):
                        for t in range(GT):
                            if s + 1 < NG:
                                add_rows(s + 1, k, t)
                            next(scale, None)
                        if k == 0 and middle:
                            kv_mask(s - 2)
                    finish(scale)
                    if 1 <= s <= NG:
                        q_sum(s - 1)
                    finish(statistics({NG: (0, 1, 2), NG + 1: (3,)}.get(s, ())))
                    if s == NG:
                        k_sum(s - 1)
                    if s == NG + 2:
                        late = statistics(range(EARLY[1], NG - 1))
                        row_scalars(ch, dve, 0, GT * EARLY[1], late)
                        finish(late)
                    if middle:
                        den_max(s - 2)
                        den_inverse(s - 2)
                        divide(s - 2)
                    if s >= 3:
                        residual(s - 3)
                finish(statistics((NG - 1,)))

        chain = [None]

        def dve_chain(dve):
            if chain[0] is None:
                chain[0] = Chain(dve, dve_step)
            chain[0].eng = dve
            return chain[0]

        act_steps = [None]

        def act_chain(act):
            if act_steps[0] is None:
                act_steps[0] = Chain(act, act_step)
            act_steps[0].eng = act
            return act_steps[0]

        with ExitStack() as stage, nc.Block() as block:
            route = Route(0, stage)
            wexp_raw = scoped(stage, "wexp_raw", [P, RB, 2, H])
            wraw = scoped(stage, "wraw", [P, 4, C])
            brows = scoped(stage, "brows", [NBIAS, P])

            def load_expert(eng, e):
                eng.dma_start(wexp_raw[:, e % RB, 0], w1[e]).then_inc(exp_raw_in[e], 16)
                eng.dma_start(wexp_raw[:, e % RB, 1].rearrange("p (c m) -> p c m", m=C), w2[e].rearrange("(c p) m -> p c m", p=P)).then_inc(exp_raw_in[e], 16)

            @block.sync
            def _(sp):
                for g in range(NG):
                    if g >= 4:
                        sp.wait_ge(x_arrived[g % 4], 16)
                    sp.dma_start(x_sb[:, g * GT:(g + 1) * GT, :], rows(xf, g * SEQ)).then_inc(x_arrived[g % 4], 16)
                for e in range(RB):
                    load_expert(sp, e)
                route.sync(sp)

            @block.gpsimd
            def _(gp):
                ch = Chain(gp, const_chain)
                ch.add(nc.gpsimd.memset(ident[:], 0.0))
                ch.add(nc.gpsimd.memset(tri[:], 1.0))
                ch.add(nc.gpsimd.memset(head_mask[:], 1.0))
                ch.add(nc.gpsimd.memset(ones_row[:], 1.0))
                ch.add(nc.gpsimd.memset(part01[:], 0.0))
                ch.add(nc.gpsimd.memset(ones_bf[:], 1.0))
                ch.then(nc.gpsimd.memset(carry[:], 1.0))
                fl = dict(allow_small_or_imprecise_dtypes=True)
                ch.add(nc.gpsimd.affine_select(out=ident[:], in_=ident[:], compare_op=ALU.not_equal, fill=1.0, base=0, pattern=[[-1, P]], channel_multiplier=1))
                ch.add(nc.gpsimd.affine_select(out=tri[:], in_=tri[:], compare_op=ALU.is_ge, fill=0.0, base=0, pattern=[[1, P]], channel_multiplier=-1))
                ch.add(nc.gpsimd.affine_select(out=part01[:], in_=part01[:], compare_op=ALU.not_equal, fill=1.0, base=0, pattern=[[-1, 2]], channel_multiplier=1))
                ch.add(nc.gpsimd.memset(carry[:, :, 0:1], 0.0))
                ch.then(nc.gpsimd.affine_select(out=head_mask[:], in_=head_mask[:], compare_op=ALU.is_ge, fill=0.0, base=0, pattern=[[-HD, HEADS]], channel_multiplier=1))
                ch.then(nc.gpsimd.affine_select(out=head_mask[:], in_=head_mask[:], compare_op=ALU.is_ge, fill=0.0, base=HD - 1, pattern=[[HD, HEADS]], channel_multiplier=-1))
                ch.add(nc.gpsimd.tensor_copy(block_mask[:].rearrange("p (h d) -> p h d", d=HD), head_mask[:].unsqueeze(2).to_broadcast([P, HEADS, HD])))
                ch.add(nc.gpsimd.iota(iota_lo[:], pattern=[[1, P]], base=0, channel_multiplier=0, **fl))
                ch.add(nc.gpsimd.iota(prefer[:], pattern=[[-1, E]], base=E, channel_multiplier=0, **fl))
                ch.add(nc.gpsimd.iota(iota_hi[:], pattern=[[P, NCH]], base=0, channel_multiplier=0, **fl))
                ch.add(nc.gpsimd.iota(expert_base[:], pattern=[[CAP, E]], base=0, channel_multiplier=0, **fl))
                ch.then(nc.gpsimd.iota(token_id[:], pattern=[[P, NT]], base=0, channel_multiplier=1, **fl))
                nc.gpsimd.tensor_copy(ones2[:], ones_row[:]).then_inc(consts, 1)
                for j, W in enumerate((Wq, Wk, Wv, Wo)):
                    gp.dma_start(wraw[:, j], W).then_inc(small_in[0], 16)
                gp.dma_start(brows[0:E * HC], b1.rearrange("e (c p) -> (e c) p", p=P)).then_inc(small_in[1], 16)
                gp.dma_start(brows[E * HC:E * HC + E], b2).then_inc(small_in[1], 16)
                gp.dma_start(brows[NBIAS - 1:NBIAS], bq.rearrange("(a n) -> a n", a=1)).then_inc(small_in[1], 16)
                for j, bias in enumerate((bk, bv, bo)):
                    gp.dma_start(brow[:, j], bias.rearrange("(a n) -> a n", a=1).to_broadcast([2, C])).then_inc(small_in[1], 16)
                for e in range(E):
                    if e == E - 2:
                        route.gpsimd_columns(gp)
                    gp.wait_ge(exp_hi, e + 1)
                    nc.gpsimd.tensor_tensor(wres[:, e, 2:4], wexp_raw[:, e % RB], wres[:, e, 0:2].bitcast(F32), ALU.subtract).then_inc(exp_lo, 1)

            @block.scalar
            def _(act):
                act.dma_start(wg_sb[:], wg).then_inc(small_in[2], 16)
                def high_part(e):
                    act.wait_ge(exp_raw_in[e], 32)
                    nc.scalar.copy(wres[:, e, 0:2], wexp_raw[:, e % RB]).then_inc(exp_hi, 1)

                route.scalar_norm(act, lambda g: high_part(g - 1) if 1 <= g <= RB else None)
                act.wait_ge(WT_ps, 1)
                nc.scalar.copy(WT[:].rearrange("p w c -> p (w c)"), bank[4][:]).then_inc(WT_sb, 1)
                by_expert = bcol[:, 0:E * (HC + 1)].rearrange("p (e c) -> p e c", c=HC + 1)
                nc.scalar.copy(by_expert[:, :, 0:HC], bank[5][:, 0:E * HC].rearrange("p (e c) -> p e c", c=HC))
                nc.scalar.copy(by_expert[:, :, HC], bank[5][:, E * HC:E * HC + E])
                nc.scalar.copy(bcol[:, NBIAS - 1:NBIAS], bank[5][:, NBIAS - 1:NBIAS])
                nc.scalar.mul(nbq[:], bank[5][:, NBIAS - 1:NBIAS], -1.0).then_inc(WT_sb, 1)
                for e in range(RB, E):
                    high_part(e)
                route.scalar_gate(act)
                route.scalar_rows(act, act_chain(act))

            @block.tensor
            def _(pe):
                pe.wait_ge(consts, 1)
                pe.wait_ge(small_in[2], 16)
                route.tensor(pe)

            @block.vector
            def _(dve):
                ch = dve_chain(dve)
                finish(row_statistics(ch, dve, range(EARLY[0])))
                late = row_statistics(ch, dve, range(EARLY[0], NG))
                row_scalars(ch, dve, 0, GT * EARLY[0], late)
                finish(late)
                route.vector(dve, ch)

        def experts_block(f):
            with ExitStack() as stage, nc.Block() as block:
                experts = Experts(f, stage)

                @block.sync
                def _(sp):
                    experts.sync(sp)

                @block.gpsimd
                def _(gp):
                    experts.gpsimd(gp)

                @block.tensor
                def _(pe):
                    experts.tensor(pe)

                @block.scalar
                def _(act):
                    experts.scalar(act)

                @block.vector
                def _(dve):
                    experts.vector(dve)

        experts_block(0)

        with ExitStack() as stage, nc.Block() as block:
            gather = Gather(stage, 0)
            attention = Attention(stage, gather)

            @block.gpsimd
            def _(gp):
                nc.gpsimd.memset(attention.vv[:, :, :, C:C + 1], 1.0).then_inc(ones_col, 1)
                gather.gpsimd(gp)

            @block.tensor
            def _(pe):
                attention.tensor(pe)

            @block.scalar
            def _(act):
                attention.scalar(act)

            @block.vector
            def _(dve):
                attention.vector(dve, dve_chain(dve))

        with ExitStack() as stage, nc.Block() as block:
            route = Route(1, stage)

            @block.sync
            def _(sp):
                route.sync(sp)

            @block.scalar
            def _(act):
                route.scalar_norm(act)
                route.scalar_gate(act)
                route.scalar_rows(act, act_chain(act))

            @block.gpsimd
            def _(gp):
                route.gpsimd_columns(gp)

            @block.tensor
            def _(pe):
                route.tensor(pe)

            @block.vector
            def _(dve):
                route.vector(dve, dve_chain(dve))

        experts_block(1)

        with ExitStack() as stage, nc.Block() as block:
            gather = Gather(stage, 1)
            last = scoped(stage, "last", [P, 2, GT, C])

            @block.gpsimd
            def _(gp):
                gather.gpsimd(gp)

            @block.vector
            def _(dve):
                for n in range(NG):
                    u = n % 2
                    for k in range(K):
                        dve.wait_ge(yg_in[2 * u + k], 64 * ((NG + n) // 2 + 1))
                        if k == 1:
                            dve.wait_ge(yg_used[0], NG + n + 1)
                        elif n >= 2:
                            dve.wait_ge(out_stored[u], 16 * (n // 2))
                        for t in range(GT):
                            at = GT * n + t
                            one = dve.scalar_tensor_tensor(last[:, u, t], gather.yg[:, u, k, t], gate[:, k, at:at + 1],
                                                           x_sb[:, at] if k == 0 else last[:, u, t], ALU.mult, ALU.add)
                        one.then_inc(yg_used[k], 1)

            @block.sync
            def _(sp):
                for n in range(NG):
                    sp.wait_ge(yg_used[1], NG + n + 1)
                    sp.dma_start(rows(of, n * SEQ), last[:, n % 2]).then_inc(out_stored[n % 2], 16)
                for u in range(2):
                    sp.wait_ge(out_stored[u], 16 * NG // 2)


_INS = ["L0_attn_x", "L0_attn_Wq", "L0_attn_bq", "L0_attn_Wk", "L0_attn_bk", "L0_attn_Wv", "L0_attn_bv", "L0_attn_Wo",
        "L0_attn_bo", "L0_ffn_wg", "L0_ffn_w1", "L0_ffn_b1", "L0_ffn_w2", "L0_ffn_b2"]
_OUTS = [((8, 512, 128), "float32")]


def kernel(**inputs):
    import numpy as _np
    import concourse.bacc as _bacc
    from concourse import mybir as _mybir
    from concourse.bass_utils import run_bass_kernel_spmd as _run

    nc = _bacc.Bacc("TRN2", target_bir_lowering=False, num_devices=1)
    arrays, args = {}, []
    for name in _INS:
        a = _np.ascontiguousarray(inputs[name])
        arrays[f"in_{name}"] = a
        args.append(nc.dram_tensor(f"in_{name}", a.shape, _mybir.dt.from_np(a.dtype), kind="ExternalInput").ap())
    for i, (shape, dtype) in enumerate(_OUTS):
        args.append(nc.dram_tensor(f"out_{i}", shape, _mybir.dt.from_np(_np.dtype(dtype)), kind="ExternalOutput").ap())
    macaron(nc, *args)
    r = _run(nc, [arrays], core_ids=[0])
    return r.results[0]["out_0"]
```
